# Optimizing a Trainium2 kernel written in Bass

```python
import numpy as np
import jax
import jax.numpy as jnp

def _softmax(x, axis=-1):
    return jax.nn.softmax(x, axis=axis)
def _gelu(x):
    return jax.nn.gelu(x, approximate=True)
def _silu(x):
    return jax.nn.silu(x)
def _sigmoid(x):
    return jax.nn.sigmoid(x)
def _layernorm(x, axis=-1, eps=1e-5):
    m = jnp.mean(x, axis=axis, keepdims=True)
    v = jnp.var(x, axis=axis, keepdims=True)
    return (x - m) / jnp.sqrt(v + eps)
def _scatter_add(tgt, idx, src, axis=0):
    return tgt.at[idx].add(src)
def _segment_sum(src, seg, n):
    return jax.ops.segment_sum(src, seg, n)

kernel_name = 'mk_adj_preln_d1_adj_512_a08dc8'

def setup_inputs(seed: int = 0):
    np.random.seed(seed)
    _w = jnp.asarray
    def _rec_inputs():
        import jax
        import jax.numpy as jnp
        _gk = jax.random.key(seed)
        x = -0.0002928 + 1 * jax.random.normal(jax.random.fold_in(_gk, 1), (8, 2048, 512), jnp.float32)
        _a = jax.random.bernoulli(jax.random.fold_in(_gk, 2), 0.00195312, (8, 2048, 2048))
        _a = jnp.logical_or(_a, jnp.swapaxes(_a, -1, -2))
        _a = jnp.logical_or(_a, jnp.eye(2048, dtype=bool))
        adj = _a.astype(jnp.int32)
        return x, adj
    x, adj = _rec_inputs()
    def _L0_gnn_setup():
        import jax, jax.numpy as jnp
        import numpy as np
        NEG_SLOPE = 0.2
        key = jax.random.key(seed)
        k1, k2, k3, k4, k5 = jax.random.split(key, 5)
        B, N, H = (8, 1024, 512)
        node_features = jax.random.normal(k1, (B, N, H), dtype=jnp.float32)
        adjacency_matrix = jax.random.randint(k2, (B, N, N), 0, 2, dtype=jnp.int32)
        scale = 1.0 / np.sqrt(2 * H)
        attn_w_src = jax.random.uniform(k3, (H,), jnp.float32, -scale, scale)
        attn_w_dst = jax.random.uniform(k4, (H,), jnp.float32, -scale, scale)
        attn_b = jax.random.uniform(k5, (1,), jnp.float32, -scale, scale)
        return {'node_features': node_features, 'adjacency_matrix': adjacency_matrix, 'attn_w_src': attn_w_src, 'attn_w_dst': attn_w_dst, 'attn_b': attn_b}
    _L0_gnn_all = _L0_gnn_setup()
    _L0_gnn_in = {k: v for k, v in _L0_gnn_all.items() if k in ('attn_w_src', 'attn_w_dst', 'attn_b', )}
    del _L0_gnn_all

    return {
        "x": x,
        "adj": adj,
        "L0_gnn_attn_w_src": _L0_gnn_in["attn_w_src"],
        "L0_gnn_attn_w_dst": _L0_gnn_in["attn_w_dst"],
        "L0_gnn_attn_b": _L0_gnn_in["attn_b"],
    }

def reference(x, adj, L0_gnn_attn_w_src, L0_gnn_attn_w_dst, L0_gnn_attn_b):
    import jax
    import jax.numpy as jnp
    def _L0_gnn_ref(node_features, adjacency_matrix, attn_w_src, attn_w_dst, attn_b):
        import jax, jax.numpy as jnp
        import numpy as np
        NEG_SLOPE = 0.2
        B, N, H = node_features.shape
        s_src = jnp.einsum('bnh,h->bn', node_features, attn_w_src)
        s_dst = jnp.einsum('bnh,h->bn', node_features, attn_w_dst)
        scores = s_src[:, :, None] + s_dst[:, None, :] + attn_b[0]
        scores = jax.nn.leaky_relu(scores, negative_slope=NEG_SLOPE)
        adj = adjacency_matrix.astype(jnp.float32) + jnp.eye(N, dtype=jnp.float32)[None]
        scores = jnp.where(adj == 0, -jnp.inf, scores)
        attn = jax.nn.softmax(scores, axis=-1)
        return jnp.einsum('bij,bjh->bih', attn, node_features)

    h = jnp.maximum(_layernorm(x, axis=-1), 0.0)
    x = x + _L0_gnn_ref(h, adj, L0_gnn_attn_w_src, L0_gnn_attn_w_dst, L0_gnn_attn_b)
    return x


_drawn_inputs = setup_inputs


def setup_inputs(seed=0):
    import zlib

    import numpy as np

    out = dict(_drawn_inputs(seed))
    spreads = {}
    factors = {}
    for name, (base, spread) in spreads.items():
        noise = np.random.default_rng([zlib.crc32(name.encode()), seed]).standard_normal(out[name].shape)
        drawn = base * np.exp(spread * noise) if base else spread * noise
        out[name] = jnp.asarray(drawn.astype(out[name].dtype))
    for name, factor in factors.items():
        out[name] = (out[name] * factor).astype(out[name].dtype)
    return out
```

```python
from contextlib import ExitStack

import concourse.bass as bass
from concourse import mybir

F32 = mybir.dt.float32
F16 = mybir.dt.float16
BF16 = mybir.dt.bfloat16
I32 = mybir.dt.int32
ALU = mybir.AluOpType
ACT = mybir.ActivationFunctionType
AX = mybir.AxisListType

P = 128
SLOPE = 0.2
STEEP = 1.0 - SLOPE
EPS = 1e-5
P_SCALE = 4096.0
H_SCALE = 512.0
TINY = 2.0 ** -60
ROW_SCALE = 2.0 ** -65
LOWEST = -3.0e38


class Batch:

    def __init__(self, index, units, tiles, quarters, rows, slot, first=False):
        self.index, self.units, self.tiles, self.quarters, self.rows = index, units, tiles, quarters, rows
        self.slot = slot
        self.first = first


def gnn_layer(nc, x, adj, w_src, w_dst, attn_b, out):
    B, N, H = x.shape
    T = N // P
    WIDE = 4
    Q = T // WIDE
    I = WIDE * P
    STEPS = Q * T
    MAIN = 460
    REST = H - MAIN
    HC = H + 2
    AHEAD = 2

    x_rows = x.rearrange("b n h -> (b n) h")
    adj_rows = adj.rearrange("b i j -> (b i) j")
    out_rows = out.rearrange("b n h -> (b n) h")
    row_scratch = nc.dram_tensor("row_scratch", [B, 2 * T * P], F32, kind="Internal").ap()

    NORM_STEP = [1 + 3 * t for t in range(T)]
    ROWS_STEP = NORM_STEP[-1] + 4
    GATE_STEP = [[q * T + s for s in ((2, 5, 8, 11) if q < Q - 1 else (6, 8, 9, 11))] for q in range(Q)]

    nc.disable_value_cache = True
    with ExitStack() as ctx:
        def sb(name, shape, dt):
            return ctx.enter_context(nc.sbuf_tensor(name, shape, dt))

        def ps(name, shape, dt):
            return ctx.enter_context(nc.psum_tensor(name, shape, dt))

        def sem(name):
            return ctx.enter_context(nc.semaphore(name))

        adj_int = sb("adj_int", [P, 2, N], I32)
        mask = sb("mask", [P, 2, WIDE, N], BF16)
        gate_diag = sb("gate_diag", [P, 2, WIDE, P], BF16)
        h_hi = sb("h_hi", [P, 2, T, HC], F16)
        h_lo = sb("h_lo", [P, 2, T, HC], F16)
        x_norm = sb("x_norm", [P, 4, H], F32)
        x_res = sb("x_res", [P, WIDE, H], F32)
        out_sb = sb("out_sb", [P, WIDE, H], F32)
        h_full = sb("h_full", [P, 2, H], F32)
        prod = sb("prod", [P, 2, H], F32)
        prod_junk = sb("prod_junk", [P, 2, H], BF16)
        max_junk = sb("max_junk", [P, N], BF16)
        score = sb("score", [P, 2, I], F32)
        prob = sb("prob", [P, 2, I], F32)
        prob_hi = sb("prob_hi", [P, 4, I], F16)
        prob_lo = sb("prob_lo", [P, 4, I], F16)
        d_row = sb("d_row", [P, N], F32)
        s_row = sb("s_row", [P, 2, I], F32)
        w_src_b = sb("w_src_b", [P, H], F32)
        w_dst_b = sb("w_dst_b", [P, H], F32)
        bias_b = sb("bias_b", [P, 1], F32)
        bias_steep = sb("bias_steep", [P, 1], F32)
        ident_f = sb("ident_f", [P, P], F32)
        ident_b = sb("ident_b", [P, P], BF16)
        ident_i = sb("ident_i", [P, P], I32)
        stats = sb("stats", [P, 2, 6], F32)
        mean_var = sb("mean_var", [P, 2, 2], F32)
        var_eps = sb("var_eps", [P, 1], F32)
        minus_half = sb("minus_half", [P, 1], F32)
        rstd = sb("rstd", [P, 2], F32)
        shift = sb("shift", [P, 2], F32)
        mean_rstd = sb("mean_rstd", [P, 1], F32)
        dots = sb("dots", [P, 2 * T], F32)
        d_steep = sb("d_steep", [P, T], F32)
        s_steep = sb("s_steep", [P, T], F32)
        exp_bias = sb("exp_bias", [P, T], F32)
        d_min = sb("d_min", [P, 1], F32)
        lift_raw = sb("lift_raw", [P, 1], F32)
        lift = sb("lift", [P, 1], F32)
        rows_sb = sb("rows_sb", [2 * T, P], F32)
        row_mul = sb("row_mul", [2 * T, 1], F32)
        row_add = sb("row_add", [2 * T, 1], F32)
        d_top = sb("d_top", [P, WIDE], F32)
        d_max = sb("d_max", [P, WIDE], F32)
        w_low = sb("w_low", [P, WIDE], F32)
        w_high = sb("w_high", [P, WIDE], F32)
        w_sum = sb("w_sum", [P, WIDE], F32)
        w_pos = sb("w_pos", [P, WIDE], F32)
        w_max = sb("w_max", [P, WIDE], F32)
        gate = sb("gate", [P, WIDE], F32)
        rest_sb = sb("rest_sb", [P, WIDE, REST + 1], F32)
        inv_sum = sb("inv_sum", [P, WIDE], F32)

        acc = ps("acc", [P, WIDE, 512], F32)
        acc_rest = ps("acc_rest", [P, 512], F32)
        gate_ps = [ps(f"gate_ps{i}", [P, 512], F32) for i in range(2)]
        rows_ps = ps("rows_ps", [P, 512], F32)

        weights_loaded = sem("weights_loaded")
        adj_loaded = [sem(f"adj_loaded{i}") for i in range(2)]
        x_norm_loaded = [sem(f"x_norm_loaded{i}") for i in range(4)]
        x_res_loaded = [sem(f"x_res_loaded{i}") for i in range(WIDE)]
        stored = [sem(f"stored{i}") for i in range(WIDE)]
        rows_written = sem("rows_written")
        d_row_loaded = sem("d_row_loaded")
        s_row_loaded = [sem(f"s_row_loaded{i}") for i in range(2)]
        const_step = sem("const_step")
        consts_ready = sem("consts_ready")
        bias_scaled = sem("bias_scaled")
        stats_raw = sem("stats_raw")
        stats_ready = sem("stats_ready")
        var_ready = sem("var_ready")
        rstd_ready = sem("rstd_ready")
        mean_rstd_ready = sem("mean_rstd_ready")
        shift_ready = sem("shift_ready")
        h_full_ready = sem("h_full_ready")
        h_hi_ready = sem("h_hi_ready")
        h_lo_ready = sem("h_lo_ready")
        prod_ready = sem("prod_ready")
        dot_ready = sem("dot_ready")
        rows_turned = sem("rows_turned")
        rows_ready = sem("rows_ready")
        d_min_ready = sem("d_min_ready")
        lift_raw_ready = sem("lift_raw_ready")
        lift_ready = sem("lift_ready")
        s_steep_ready = sem("s_steep_ready")
        d_steep_ready = sem("d_steep_ready")
        exp_bias_ready = sem("exp_bias_ready")
        adj_fixed = sem("adj_fixed")
        mask_ready = sem("mask_ready")
        d_top_ready = sem("d_top_ready")
        d_max_ready = sem("d_max_ready")
        w_parts_ready = sem("w_parts_ready")
        w_sum_ready = sem("w_sum_ready")
        w_pos_ready = sem("w_pos_ready")
        w_max_ready = sem("w_max_ready")
        gate_ready = sem("gate_ready")
        gate_diag_ready = sem("gate_diag_ready")
        mask_turned = sem("mask_turned")
        score_ready = sem("score_ready")
        prob_ready = sem("prob_ready")
        prob_hi_ready = sem("prob_hi_ready")
        prob_lo_ready = sem("prob_lo_ready")
        unit_done = sem("unit_done")
        acc_ready = sem("acc_ready")
        inv_ready = sem("inv_ready")
        acc_read = sem("acc_read")
        rest_ready = sem("rest_ready")
        rest_read = sem("rest_read")

        def known_below(n, limit):
            return isinstance(n, int) and n < limit

        def batch_at(n):
            return Batch(n, STEPS * n, T * n, Q * n, N * n, n % 2, n == 0)

        def over_batches(eng, body):
            with eng.Fori(0, B // 2 - 1) as pair:
                held = [eng.snap(pair * (2 * c)) for c in (1, STEPS, T, Q, N)]
                b0, b1, b2 = (Batch(*(h + c * k for h, c in zip(held, (1, STEPS, T, Q, N))), k % 2)
                              for k in range(3))
                body(b0, b1)
                body(b1, b2)
            body(batch_at(B - 2), batch_at(B - 1))
            body(batch_at(B - 1), None)

        first = batch_at(0)

        block = ctx.enter_context(nc.Block())

        @block.sync
        def _(sp):
            def load_x_norm(nb, t):
                if nb.first:
                    if t >= 4:
                        sp.wait_ge(h_full_ready, t - 3)
                else:
                    sp.wait_ge(h_full_ready, nb.tiles + t - 3)
                sp.dma_start(x_norm[:, t % 4, :], x_rows[bass.ds(nb.rows + P * t, P), :]) \
                    .then_inc(x_norm_loaded[t % 4], 16)

            def load_adj(nb, q, k):
                if nb.first and q == 0:
                    if k >= 2:
                        sp.wait_ge(mask_ready, k - 1)
                else:
                    sp.wait_ge(mask_ready, nb.tiles + WIDE * q + k - 1)
                sp.dma_start(adj_int[:, k % 2, :], adj_rows[bass.ds(nb.rows + I * q + P * k, P), :]) \
                    .then_inc(adj_loaded[k % 2], 16)

            def load_x_res(b, q):
                for w in range(WIDE):
                    if not (b.first and q == 0):
                        sp.wait_ge(acc_read, b.tiles + WIDE * q + w + 1)
                    sp.dma_start(x_res[:, w, :], x_rows[bass.ds(b.rows + I * q + P * w, P), :]) \
                        .then_inc(x_res_loaded[w], 16)

            def store(b, q):
                for w in range(WIDE):
                    sp.wait_ge(acc_read, b.tiles + WIDE * (q + 1) + w + 1)
                    sp.dma_start(out_rows[bass.ds(b.rows + I * q + P * w, P), :], out_sb[:, w, :]) \
                        .then_inc(stored[w], 16)

            def write_rows(nb):
                sp.wait_ge(rows_ready, nb.index + 1)
                sp.dma_start(row_scratch[bass.ds(nb.index, 1), :].rearrange("a (r p) -> (a r) p", p=P), rows_sb[:, :]) \
                    .then_inc(rows_written, 16)

            def load_d_row(nb):
                sp.wait_ge(d_top_ready, nb.tiles)
                sp.wait_ge(rows_written, 16 * (nb.index + 1))
                sp.dma_start(d_row[:, :], row_scratch[bass.ds(nb.index, 1), 0:N].partition_broadcast(P)) \
                    .then_inc(d_row_loaded, 16)

            def load_s_row(b, q):
                if not (b.first and q == 0):
                    sp.wait_ge(score_ready, b.units + T * (q - 1) + 1)
                sp.wait_ge(rows_written, 16 * (b.index + 1))
                sp.dma_start(s_row[:, q % 2, :],
                             row_scratch[bass.ds(b.index, 1), N + I * q:N + I * (q + 1)].partition_broadcast(P)) \
                    .then_inc(s_row_loaded[q % 2], 16)

            sp.dma_start(w_src_b[:, :], w_src.rearrange("(a h) -> a h", a=1).partition_broadcast(P)) \
                .then_inc(weights_loaded, 16)
            sp.dma_start(w_dst_b[:, :], w_dst.rearrange("(a h) -> a h", a=1).partition_broadcast(P)) \
                .then_inc(weights_loaded, 16)
            sp.dma_start(bias_b[:, :], attn_b.rearrange("(a h) -> a h", a=1).partition_broadcast(P)) \
                .then_inc(weights_loaded, 16)
            for t in range(T):
                load_x_norm(first, t)
                if t == 4:
                    load_adj(first, 0, 0)
                    load_adj(first, 0, 1)
            write_rows(first)
            load_d_row(first)
            load_s_row(first, 0)
            load_adj(first, 0, 2)
            load_adj(first, 0, 3)
            load_x_res(first, 0)

            def steps(b, after):
                for s in range(STEPS):
                    q = s // T
                    if s % T == 1 and q > 0:
                        store(b, q - 1)
                        load_x_res(b, q)
                    for t in range(T):
                        if s == max(NORM_STEP[t] - 2, 0) and after:
                            load_x_norm(after, t)
                    if s == ROWS_STEP and after:
                        write_rows(after)
                        load_d_row(after)
                    if s == q * T + 10 and q < Q - 1:
                        load_s_row(b, q + 1)
                    if s == (Q - 1) * T + 10 and after:
                        load_s_row(after, 0)
                    for k in range(WIDE):
                        if s == GATE_STEP[q][k] - 2 and (q < Q - 1 or after):
                            if q < Q - 1:
                                load_adj(b, q + 1, k)
                            else:
                                load_adj(after, 0, k)
                store(b, Q - 1)
                if after:
                    load_x_res(after, 0)

            over_batches(sp, steps)
            for w in range(WIDE):
                sp.wait_ge(stored[w], 16 * (B * Q + 1))

        @block.gpsimd
        def _(pool):
            nc.gpsimd.memset(ident_f[:, :], 0.0).then_inc(const_step, 1)
            nc.gpsimd.memset(minus_half[:, :], -0.5).then_inc(consts_ready, 1)
            nc.gpsimd.memset(row_mul[:, :], STEEP).then_inc(const_step, 1)
            pool.wait_ge(const_step, 2)
            nc.gpsimd.memset(row_mul[0:T, :], ROW_SCALE).then_inc(consts_ready, 1)
            nc.gpsimd.affine_select(out=ident_f[:, :], in_=ident_f[:, :], compare_op=ALU.not_equal, fill=1.0,
                                    base=0, pattern=[[-1, P]], channel_multiplier=1).then_inc(const_step, 1)
            pool.wait_ge(const_step, 3)
            nc.gpsimd.tensor_copy(ident_b[:, :], ident_f[:, :]).then_inc(consts_ready, 1)
            nc.gpsimd.tensor_copy(ident_i[:, :], ident_f[:, :]).then_inc(consts_ready, 1)
            nc.gpsimd.memset(h_hi[:, :, :, H:HC], H_SCALE).then_inc(consts_ready, 1)
            pool.wait_ge(weights_loaded, 48)
            pool.nop(nofuse=True)
            nc.gpsimd.tensor_scalar(bias_steep[:, :], bias_b[:, :], STEEP, None, ALU.mult).then_inc(bias_scaled, 1)
            pool.wait_ge(bias_scaled, 1)
            nc.gpsimd.tensor_copy(row_add[:, :], bias_steep[0:2 * T, :]).then_inc(bias_scaled, 1)
            pool.wait_ge(bias_scaled, 2)
            nc.gpsimd.memset(row_add[0:T, :], 0.0).then_inc(consts_ready, 1)
            pool.wait_ge(consts_ready, 6)

            def norm_scalars(nb, t):
                n = nb.tiles + t
                pool.wait_ge(stats_ready, n + 1)
                pool.nop(nofuse=True)
                nc.gpsimd.tensor_scalar(var_eps[:, :], mean_var[:, t % 2, 1:2], EPS, H_SCALE ** -2,
                                        ALU.add, ALU.mult).then_inc(var_ready, 1)
                pool.wait_ge(var_ready, n + 1)
                nc.gpsimd.tensor_tensor(rstd[:, t % 2:t % 2 + 1], var_eps[:, :], minus_half[:, :],
                                        ALU.pow).then_inc(rstd_ready, 1)
                pool.wait_ge(rstd_ready, n + 1)
                nc.gpsimd.tensor_tensor(mean_rstd[:, :], mean_var[:, t % 2, 0:1], rstd[:, t % 2:t % 2 + 1],
                                        ALU.mult).then_inc(mean_rstd_ready, 1)
                pool.wait_ge(mean_rstd_ready, n + 1)
                pool.nop(nofuse=True)
                nc.gpsimd.tensor_scalar(shift[:, t % 2:t % 2 + 1], mean_rstd[:, :], -1.0, None,
                                        ALU.mult).then_inc(shift_ready, 1)

            def norm_products(nb, t):
                n = nb.tiles + t
                pool.wait_ge(h_full_ready, n + 1)
                for v, w in enumerate((w_dst_b, w_src_b)):
                    if not known_below(n, 1):
                        pool.wait_ge(dot_ready, 2 * n - 1 + v)
                    nc.gpsimd.tensor_tensor(prod[:, v, :], h_full[:, t % 2, :], w[:, :],
                                            ALU.mult).then_inc(prod_ready, 1)
                pool.wait_ge(h_hi_ready, n + 1)
                nc.gpsimd.tensor_tensor(h_lo[:, nb.slot, t, 0:H], h_full[:, t % 2, :],
                                        h_hi[:, nb.slot, t, 0:H], ALU.subtract).then_inc(h_lo_ready, 1)

            def batch_scalars(nb):
                pool.wait_ge(d_min_ready, nb.index + 1)
                pool.nop(nofuse=True)
                nc.gpsimd.tensor_scalar(lift_raw[:, :], d_min[:, :], -SLOPE / ROW_SCALE, 1.0,
                                        ALU.mult, ALU.add).then_inc(lift_raw_ready, 1)
                if not nb.first:
                    pool.wait_ge(gate_ready, nb.quarters)
                    pool.wait_ge(exp_bias_ready, nb.index)
                pool.wait_ge(lift_raw_ready, nb.index + 1)
                pool.nop(nofuse=True)
                nc.gpsimd.tensor_scalar(lift[:, :], lift_raw[:, :], 1.0, None, ALU.max).then_inc(lift_ready, 1)
                pool.wait_ge(dot_ready, 2 * nb.tiles + 2 * T)
                pool.nop(nofuse=True)
                nc.gpsimd.tensor_scalar(s_steep[:, :], dots[:, T:2 * T], STEEP, bias_steep[:, 0:1],
                                        ALU.mult, ALU.add).then_inc(s_steep_ready, 1)

            def fix_adj(nb, q, k):
                t = WIDE * q + k
                pool.wait_ge(adj_loaded[k % 2], 8 * nb.tiles + 16 * (t // 2 + 1))
                nc.gpsimd.tensor_tensor(adj_int[:, k % 2, t * P:(t + 1) * P], adj_int[:, k % 2, t * P:(t + 1) * P],
                                        ident_i[:, :], ALU.add).then_inc(adj_fixed, 1)

            def gates(nb, q):
                g = nb.quarters + q
                pool.wait_ge(d_top_ready, WIDE * (g + 1))
                pool.nop(nofuse=True)
                nc.gpsimd.tensor_scalar(d_max[:, :], d_top[:, :], TINY, 1.0 / ROW_SCALE,
                                        ALU.add, ALU.mult).then_inc(d_max_ready, 1)
                pool.wait_ge(d_max_ready, g + 1)
                pool.wait_ge(s_steep_ready, nb.index + 1)
                pool.nop(nofuse=True)
                nc.gpsimd.tensor_scalar(w_low[:, :], d_max[:, :], SLOPE, None, ALU.mult).then_inc(w_parts_ready, 1)
                nc.gpsimd.tensor_scalar(w_high[:, :], d_max[:, :], STEEP, None, ALU.mult).then_inc(w_parts_ready, 1)
                pool.wait_ge(w_parts_ready, 2 * (g + 1))
                nc.gpsimd.tensor_tensor(w_sum[:, :], w_high[:, :], s_steep[:, WIDE * q:WIDE * (q + 1)],
                                        ALU.add).then_inc(w_sum_ready, 1)
                pool.wait_ge(w_sum_ready, g + 1)
                pool.nop(nofuse=True)
                nc.gpsimd.tensor_scalar(w_pos[:, :], w_sum[:, :], 0.0, None, ALU.max).then_inc(w_pos_ready, 1)
                pool.wait_ge(w_pos_ready, g + 1)
                nc.gpsimd.tensor_tensor(w_max[:, :], w_low[:, :], w_pos[:, :], ALU.add).then_inc(w_max_ready, 1)
                pool.wait_ge(w_max_ready, g + 1)
                pool.wait_ge(lift_ready, nb.index + 1)
                pool.nop(nofuse=True)
                nc.gpsimd.tensor_scalar(gate[:, :], w_max[:, :], lift[:, 0:1], -1.0 / TINY,
                                        ALU.add, ALU.mult).then_inc(gate_ready, 1)
                pool.wait_ge(gate_ready, g + 1)
                if not known_below(g, 2):
                    pool.wait_ge(mask_turned, T * (g - 1) + 1)
                pool.nop(nofuse=True)
                for k in range(WIDE):
                    nc.gpsimd.tensor_scalar(gate_diag[:, q % 2, k, :], ident_b[:, :], gate[:, k:k + 1], None,
                                            ALU.mult).then_inc(gate_diag_ready, 1)

            for t in range(T):
                norm_scalars(first, t)
                norm_products(first, t)
            batch_scalars(first)
            for k in range(WIDE):
                fix_adj(first, 0, k)
            gates(first, 0)

            def steps(b, after):
                for s in range(STEPS):
                    q = s // T
                    nq, nb = (q + 1, b) if q < Q - 1 else (0, after)
                    if after:
                        for t in range(T):
                            if s == NORM_STEP[t]:
                                norm_scalars(after, t)
                            if s == NORM_STEP[t] + 1:
                                norm_products(after, t)
                        if s == ROWS_STEP + 3:
                            batch_scalars(after)
                    if nq > 0 or after:
                        for k in range(WIDE):
                            if s == GATE_STEP[q][k] - 1:
                                fix_adj(nb, nq, k)
                        if s == GATE_STEP[q][-1]:
                            gates(nb, nq)

            over_batches(pool, steps)

        @block.scalar
        def _(act):
            def normalise(nb, t):
                n = nb.tiles + t
                act.wait_ge(x_norm_loaded[t % 4], 4 * nb.tiles + 16 * (t // 4 + 1))
                act.wait_ge(shift_ready, n + 1)
                if not known_below(n, 2):
                    act.wait_ge(h_lo_ready, n - 1)
                nc.scalar.activation(h_full[:, t % 2, :], x_norm[:, t % 4, :], ACT.Relu,
                                     bias=shift[:, t % 2:t % 2 + 1],
                                     scale=rstd[:, t % 2:t % 2 + 1]).then_inc(h_full_ready, 1)
                act.wait_ge(h_full_ready, n + 1)
                if not nb.first:
                    act.wait_ge(unit_done, nb.units - STEPS + 1)
                nc.scalar.activation(h_hi[:, nb.slot, t, 0:H], h_full[:, t % 2, :],
                                     ACT.Copy).then_inc(h_hi_ready, 1)

            def sum_products(nb, t):
                n = nb.tiles + t
                for v in range(2):
                    act.wait_ge(prod_ready, 2 * n + v + 1)
                    if t == 0 and v == 0 and not nb.first:
                        act.wait_ge(rows_turned, nb.index)
                        act.wait_ge(s_steep_ready, nb.index)
                        act.wait_ge(d_steep_ready, nb.index)
                        act.wait_ge(exp_bias_ready, nb.index)
                    nc.scalar.activation(prod_junk[:, v, :], prod[:, v, :], ACT.Copy, scale=1.0 / H_SCALE,
                                         accum_out=dots[:, v * T + t:v * T + t + 1]).then_inc(dot_ready, 1)

            def set_exp_bias(nb):
                if not nb.first:
                    act.wait_ge(prob_ready, nb.units)
                act.wait_ge(lift_ready, nb.index + 1)
                act.wait_ge(dot_ready, 2 * nb.tiles + 2 * T)
                nc.scalar.activation(exp_bias[:, :], dots[:, 0:T], ACT.Identity,
                                     bias=lift[:, 0:1]).then_inc(exp_bias_ready, 1)

            def probabilities(b, s):
                u = b.units + s
                j = s % T
                act.wait_ge(score_ready, u + 1)
                if s == 0:
                    act.wait_ge(exp_bias_ready, b.index + 1)
                if not known_below(u, 2):
                    act.wait_ge(prob_lo_ready, u - 1)
                nc.scalar.activation(prob[:, s % 2, :], score[:, s % 2, :], ACT.Exp,
                                     bias=exp_bias[:, j:j + 1]).then_inc(prob_ready, 1)
                act.wait_ge(prob_ready, u + 1)
                nc.scalar.activation(prob_hi[:, s % 4, :], prob[:, s % 2, :], ACT.Copy,
                                     scale=P_SCALE).then_inc(prob_hi_ready, 1)

            for t in range(T):
                normalise(first, t)
                sum_products(first, t)
            set_exp_bias(first)
            for s in range(AHEAD):
                probabilities(first, s)

            def steps(b, after):
                for s in range(STEPS):
                    a = s + AHEAD
                    if a == STEPS and after:
                        set_exp_bias(after)
                    if a < STEPS or after:
                        probabilities(b if a < STEPS else after, a % STEPS)
                    if after:
                        for t in range(T):
                            if s == NORM_STEP[t] + 1:
                                normalise(after, t)
                            if s == NORM_STEP[t] + 2:
                                sum_products(after, t)

            over_batches(act, steps)

        @block.vector
        def _(dve):
            def norm_stats(nb, t):
                n = nb.tiles + t
                dve.wait_ge(x_norm_loaded[t % 4], 4 * nb.tiles + 16 * (t // 4 + 1))
                nc.vector.bn_stats(stats[:, t % 2, :], x_norm[:, t % 4, :]).then_inc(stats_raw, 1)
                dve.wait_ge(stats_raw, n + 1)
                if not known_below(n, 2):
                    dve.wait_ge(shift_ready, n - 1)
                dve.nop(nofuse=True)
                nc.vector.bn_aggr(mean_var[:, t % 2, :], stats[:, t % 2, :]).then_inc(stats_ready, 1)

            def take_rows(nb):
                dve.wait_ge(consts_ready, 6)
                dve.wait_ge(rows_turned, nb.index + 1)
                if not nb.first:
                    dve.wait_ge(rows_written, 16 * nb.index)
                nc.vector.tensor_scalar(rows_sb[:, :], rows_ps[0:2 * T, 0:P], row_mul[:, 0:1], row_add[:, 0:1],
                                        ALU.mult, ALU.add).then_inc(rows_ready, 1)

            def take_d_min(nb):
                dve.wait_ge(d_row_loaded, 16 * (nb.index + 1))
                if not nb.first:
                    dve.wait_ge(lift_raw_ready, nb.index)
                nc.vector.tensor_reduce(d_min[:, :], d_row[:, :], AX.X, ALU.min).then_inc(d_min_ready, 1)

            def mask_and_max(nb, q, k):
                t = WIDE * q + k
                n = nb.tiles + t
                g = nb.quarters + q
                dve.wait_ge(adj_fixed, n + 1)
                if not known_below(g, 2):
                    dve.wait_ge(mask_turned, T * (g - 1) + 1)
                nc.vector.tensor_scalar(mask[:, q % 2, k, :], adj_int[:, k % 2, :], 0.0, TINY,
                                        ALU.is_equal, ALU.max).then_inc(mask_ready, 1)
                dve.wait_ge(mask_ready, n + 1)
                dve.wait_ge(d_row_loaded, 16 * (nb.index + 1))
                if not known_below(g, 1):
                    dve.wait_ge(d_max_ready, g)
                if not known_below(n, 1):
                    dve.wait_ge(d_top_ready, n)
                dve.nop(nofuse=True)
                nc.vector.tensor_tensor_reduce(max_junk[:, :], d_row[:, :], mask[:, q % 2, k, :], 1.0, LOWEST,
                                               ALU.subtract, ALU.max, d_top[:, k:k + 1]).then_inc(d_top_ready, 1)

            def set_d_steep(nb):
                if not nb.first:
                    dve.wait_ge(score_ready, nb.units)
                dve.wait_ge(dot_ready, 2 * nb.tiles + 2 * T)
                nc.vector.tensor_scalar(d_steep[:, :], dots[:, 0:T], -STEEP, None,
                                        ALU.mult).then_inc(d_steep_ready, 1)

            def scores(b, s):
                u = b.units + s
                q, j = s // T, s % T
                if s == 0:
                    dve.wait_ge(d_steep_ready, b.index + 1)
                if j == 0:
                    dve.wait_ge(s_row_loaded[q % 2], 8 * b.quarters + 16 * (q // 2 + 1))
                dve.wait_ge(mask_turned, u + 1)
                if not known_below(u, 2):
                    dve.wait_ge(prob_ready, u - 1)
                nc.vector.scalar_tensor_tensor(score[:, s % 2, :], s_row[:, q % 2, :], d_steep[:, j:j + 1],
                                               gate_ps[s % 2][:, 0:I], ALU.max, ALU.add).then_inc(score_ready, 1)

            def low_halves(b, s):
                u = b.units + s
                dve.wait_ge(prob_hi_ready, u + 1)
                nc.vector.scalar_tensor_tensor(prob_lo[:, s % 4, :], prob[:, s % 2, :], P_SCALE,
                                               prob_hi[:, s % 4, :], ALU.mult,
                                               ALU.subtract).then_inc(prob_lo_ready, 1)

            def take_rest(b, q):
                g = b.quarters + q
                dve.wait_ge(rest_ready, g + 1)
                dve.wait_ge(acc_read, WIDE * g + WIDE)
                nc.vector.tensor_copy(rest_sb[:, :, :], acc_rest[:, 0:WIDE * (REST + 1)]
                                      .rearrange("p (w c) -> p w c", w=WIDE)).then_inc(rest_read, 1)
                dve.wait_ge(rest_read, g + 2)
                nc.vector.reciprocal(inv_sum[:, :], rest_sb[:, :, REST]).then_inc(inv_ready, 1)

            def finish(b, q, w):
                if w < WIDE - 1:
                    dve.wait_ge(acc_ready, (WIDE - 1) * b.quarters + (WIDE - 1) * q + w + 1)
                else:
                    dve.wait_ge(unit_done, b.units + T * (q + 1))
                if w == 0:
                    dve.wait_ge(inv_ready, b.quarters + q + 1)
                dve.wait_ge(x_res_loaded[w], 16 * b.quarters + 16 * (q + 1))
                dve.wait_ge(stored[w], 16 * b.quarters + 16 * (q + 1))
                nc.vector.scalar_tensor_tensor(out_sb[:, w, MAIN:H], rest_sb[:, w, 0:REST], inv_sum[:, w:w + 1],
                                               x_res[:, w, MAIN:H], ALU.mult, ALU.add)
                nc.vector.scalar_tensor_tensor(out_sb[:, w, 0:MAIN], acc[:, w, 0:MAIN], inv_sum[:, w:w + 1],
                                               x_res[:, w, 0:MAIN], ALU.mult, ALU.add).then_inc(acc_read, 1)

            dve.sem_inc(acc_read, WIDE)
            dve.sem_inc(rest_read, 1)
            for w in range(WIDE):
                dve.sem_inc(stored[w], 16)
            for t in range(T):
                norm_stats(first, t)
            take_rows(first)
            set_d_steep(first)
            take_d_min(first)
            for k in range(WIDE):
                mask_and_max(first, 0, k)
            scores(first, 0)
            scores(first, 1)
            low_halves(first, 0)

            def steps(b, after):
                for s in range(STEPS):
                    q = s // T
                    nq, nb = (q + 1, b) if q < Q - 1 else (0, after)
                    a = s + AHEAD
                    if s % T == 0 and q > 0:
                        finish(b, q - 1, WIDE - 1)
                    if a == STEPS and after:
                        set_d_steep(after)
                    if a < STEPS or after:
                        scores(b if a < STEPS else after, a % STEPS)
                    if a - 1 < STEPS or after:
                        low_halves(b if a - 1 < STEPS else after, (a - 1) % STEPS)
                    if after:
                        for t in range(T):
                            if s == NORM_STEP[t]:
                                norm_stats(after, t)
                        if s == ROWS_STEP:
                            take_rows(after)
                        if s == ROWS_STEP + 3:
                            take_d_min(after)
                    if nq > 0 or after:
                        for k in range(WIDE):
                            if s == GATE_STEP[q][k]:
                                mask_and_max(nb, nq, k)
                    if s % T == T - 1:
                        take_rest(b, q)
                        for w in range(WIDE - 1):
                            finish(b, q, w)
                finish(b, Q - 1, WIDE - 1)

            over_batches(dve, steps)

        @block.tensor
        def _(pe):
            def turn_rows(nb):
                pe.wait_ge(dot_ready, 2 * nb.tiles + 2 * T)
                if not nb.first:
                    pe.wait_ge(rows_ready, nb.index)
                nc.tensor.transpose(rows_ps[0:2 * T, 0:P], dots[:, :], ident_f[:, :]).then_inc(rows_turned, 1)

            def turn_masks(b, s):
                u = b.units + s
                q, j = s // T, s % T
                if j == 0:
                    pe.wait_ge(gate_diag_ready, b.tiles + WIDE * (q + 1))
                    pe.wait_ge(mask_ready, b.tiles + WIDE * (q + 1))
                if not known_below(u, 2):
                    pe.wait_ge(score_ready, u - 1)
                for k in range(WIDE):
                    last = nc.tensor.matmul(gate_ps[s % 2][:, k * P:(k + 1) * P],
                                            mask[:, q % 2, k, j * P:(j + 1) * P], gate_diag[:, q % 2, k, :],
                                            start=True, stop=True)
                last.then_inc(mask_turned, 1)

            def multiply(b, s):
                u = b.units + s
                q, j = s // T, s % T
                if s == 0:
                    pe.wait_ge(h_lo_ready, b.tiles + T)
                pe.wait_ge(prob_hi_ready, u + 1)
                pe.wait_ge(prob_lo_ready, u + 1)
                hi = h_hi[:, b.slot, j, :]
                lo = h_lo[:, b.slot, j, :]
                start, stop = j == 0, j == T - 1
                if start:
                    pe.wait_ge(rest_read, b.quarters + q + 1)
                for w in range(WIDE):
                    p_hi = prob_hi[:, s % 4, w * P:(w + 1) * P]
                    p_lo = prob_lo[:, s % 4, w * P:(w + 1) * P]
                    c = w * (REST + 1)
                    rest = acc_rest[:, c:c + REST + 1]
                    nc.tensor.matmul(rest, p_hi, hi[:, MAIN:H + 1], start=start and w == 0, stop=False,
                                     skip_group_check=True)
                    nc.tensor.matmul(acc_rest[:, c:c + REST], p_hi, lo[:, MAIN:H], start=False, stop=False,
                                     skip_group_check=True)
                    last = nc.tensor.matmul(rest, p_lo, hi[:, MAIN:H + 1], start=False, stop=stop,
                                            skip_group_check=True)
                if stop:
                    last.then_inc(rest_ready, 1)
                for w in range(WIDE):
                    if start:
                        pe.wait_ge(acc_read, b.tiles + WIDE * q + w + 1)
                    p_hi = prob_hi[:, s % 4, w * P:(w + 1) * P]
                    p_lo = prob_lo[:, s % 4, w * P:(w + 1) * P]
                    main = acc[:, w, 0:MAIN]
                    nc.tensor.matmul(main, p_hi, hi[:, 0:MAIN], start=start, stop=False)
                    nc.tensor.matmul(main, p_hi, lo[:, 0:MAIN], start=False, stop=False)
                    last = nc.tensor.matmul(main, p_lo, hi[:, 0:MAIN], start=False, stop=stop)
                    if stop and w < WIDE - 1:
                        last.then_inc(acc_ready, 1)
                last.then_inc(unit_done, 1)

            pe.wait_ge(consts_ready, 6)
            turn_rows(first)
            turn_masks(first, 0)
            turn_masks(first, 1)

            def steps(b, after):
                for s in range(STEPS):
                    a = s + AHEAD
                    if s == ROWS_STEP and after:
                        turn_rows(after)
                    if a < STEPS or after:
                        turn_masks(b if a < STEPS else after, a % STEPS)
                    multiply(b, s)

            over_batches(pe, steps)


_INS = ["x", "adj", "L0_gnn_attn_w_src", "L0_gnn_attn_w_dst", "L0_gnn_attn_b"]


def kernel(**inputs):
    import numpy as _np
    import concourse.bacc as _bacc
    from concourse import mybir as _mybir
    from concourse.bass_utils import run_bass_kernel_spmd as _run

    nc = _bacc.Bacc("TRN2", target_bir_lowering=False, num_devices=1)
    arrays, args = {}, []
    for name in _INS:
        a = _np.ascontiguousarray(inputs[name])
        arrays[f"in_{name}_dram"] = a
        args.append(nc.dram_tensor(f"in_{name}_dram", a.shape, _mybir.dt.from_np(a.dtype), kind="ExternalInput").ap())
    x = arrays["in_x_dram"]
    args.append(nc.dram_tensor("out_0_dram", x.shape, _mybir.dt.from_np(x.dtype), kind="ExternalOutput").ap())
    gnn_layer(nc, *args)
    r = _run(nc, [arrays], core_ids=[0])
    return r.results[0]["out_0_dram"]
```

```python
from contextlib import ExitStack

import concourse.bass as bass
from concourse import mybir

F32 = mybir.dt.float32
F16 = mybir.dt.float16
BF16 = mybir.dt.bfloat16
I32 = mybir.dt.int32
ALU = mybir.AluOpType
ACT = mybir.ActivationFunctionType
AX = mybir.AxisListType

P = 128
SLOPE = 0.2
STEEP = 1.0 - SLOPE
EPS = 1e-5
P_SCALE = 4096.0
H_SCALE = 512.0
TINY = 2.0 ** -60
ROW_SCALE = 2.0 ** -65
LOWEST = -3.0e38


class Batch:

    def __init__(self, index, units, tiles, quarters, rows, slot, first=False, last=False):
        self.index, self.units, self.tiles, self.quarters, self.rows = index, units, tiles, quarters, rows
        self.slot = slot
        self.first = first
        self.last = last


def gnn_layer(nc, x, adj, w_src, w_dst, attn_b, out):
    B, N, H = x.shape
    T = N // P
    WIDE = 4
    Q = T // WIDE
    I = WIDE * P
    STEPS = Q * T
    MAIN = 460
    REST = H - MAIN
    HC = H + 2
    AHEAD = 2

    x_rows = x.rearrange("b n h -> (b n) h")
    adj_rows = adj.rearrange("b i j -> (b i) j")
    out_rows = out.rearrange("b n h -> (b n) h")
    row_scratch = nc.dram_tensor("row_scratch", [B, 2 * T * P], F32, kind="Internal").ap()

    HALVES = 2
    PER_QUARTER = 6
    NORM_STEP = [T * (t // PER_QUARTER) + 1 + 2 * (t % PER_QUARTER) for t in range(T)]
    SUM_STEP = [s + 3 if s % T < T - 5 else s + 5 for s in NORM_STEP]
    ROWS_STEP = SUM_STEP[-1] + 2
    D_MIN_STEP = (Q - 1) * T
    MASK_STEP = [[q * T + 3 * k for k in range(WIDE)] for q in range(Q)]
    TOP_STEP = [[[s + 1 + h for h in range(HALVES)] for s in MASK_STEP[q]] for q in range(Q)]
    MASK_STEP[Q - 1][0] = D_MIN_STEP - 2
    GATE_STEP = [TOP_STEP[q][WIDE - 1][HALVES - 1] for q in range(Q)]

    nc.disable_value_cache = True
    with ExitStack() as ctx:
        def sb(name, shape, dt):
            return ctx.enter_context(nc.sbuf_tensor(name, shape, dt))

        def ps(name, shape, dt):
            return ctx.enter_context(nc.psum_tensor(name, shape, dt))

        def sem(name):
            return ctx.enter_context(nc.semaphore(name))

        adj_int = sb("adj_int", [P, 2, N], I32)
        mask = sb("mask", [P, 2, WIDE, N], BF16)
        gate_diag = sb("gate_diag", [P, 2, WIDE, P], BF16)
        h_hi = sb("h_hi", [P, 2, T, HC], F16)
        h_lo = sb("h_lo", [P, 2, T, HC], F16)
        x_norm = sb("x_norm", [P, 4, H], F32)
        x_res = sb("x_res", [P, WIDE, H], F32)
        out_sb = sb("out_sb", [P, WIDE, H], F32)
        h_full = sb("h_full", [P, 2, H], F32)
        prod = sb("prod", [P, 2, H], F32)
        prod_junk = sb("prod_junk", [P, 2, H], BF16)
        max_junk = sb("max_junk", [P, N], BF16)
        score = sb("score", [P, 2, I], F32)
        prob = sb("prob", [P, 2, I], F32)
        prob_hi = sb("prob_hi", [P, 4, I], F16)
        prob_lo = sb("prob_lo", [P, 4, I], F16)
        d_row = sb("d_row", [P, N], F32)
        s_row = sb("s_row", [P, 2, I], F32)
        w_src_b = sb("w_src_b", [P, H], F32)
        w_dst_b = sb("w_dst_b", [P, H], F32)
        bias_b = sb("bias_b", [P, 1], F32)
        bias_steep = sb("bias_steep", [P, 1], F32)
        ident_f = sb("ident_f", [P, P], F32)
        ident_b = sb("ident_b", [P, P], BF16)
        ident_i = sb("ident_i", [P, P], I32)
        stats = sb("stats", [P, 2, 6], F32)
        mean_var = sb("mean_var", [P, 2, 2], F32)
        var_eps = sb("var_eps", [P, 1], F32)
        minus_half = sb("minus_half", [P, 1], F32)
        rstd = sb("rstd", [P, 2], F32)
        shift = sb("shift", [P, 2], F32)
        mean_rstd = sb("mean_rstd", [P, 1], F32)
        dots = sb("dots", [P, 2 * T], F32)
        d_steep = sb("d_steep", [P, T], F32)
        s_steep = sb("s_steep", [P, T], F32)
        exp_bias = sb("exp_bias", [P, T], F32)
        d_min = sb("d_min", [P, 1], F32)
        lift_raw = sb("lift_raw", [P, 1], F32)
        lift = sb("lift", [P, 1], F32)
        rows_sb = sb("rows_sb", [2 * T, P], F32)
        row_mul = sb("row_mul", [2 * T, 1], F32)
        row_add = sb("row_add", [2 * T, 1], F32)
        d_part = sb("d_part", [P, HALVES, WIDE], F32)
        d_top = sb("d_top", [P, WIDE], F32)
        d_max = sb("d_max", [P, WIDE], F32)
        w_low = sb("w_low", [P, WIDE], F32)
        w_high = sb("w_high", [P, WIDE], F32)
        w_sum = sb("w_sum", [P, WIDE], F32)
        w_pos = sb("w_pos", [P, WIDE], F32)
        w_max = sb("w_max", [P, WIDE], F32)
        gate = sb("gate", [P, WIDE], F32)
        rest_sb = sb("rest_sb", [P, WIDE, REST], F32)
        inv_sum = sb("inv_sum", [P, WIDE], F32)

        acc = ps("acc", [P, WIDE, 512], F32)
        acc_rest = ps("acc_rest", [P, 512], F32)
        gate_ps = [ps(f"gate_ps{i}", [P, 512], F32) for i in range(2)]
        rows_ps = ps("rows_ps", [P, 512], F32)

        weights_loaded = sem("weights_loaded")
        adj_loaded = [sem(f"adj_loaded{i}") for i in range(2)]
        x_norm_loaded = [sem(f"x_norm_loaded{i}") for i in range(4)]
        x_res_loaded = [sem(f"x_res_loaded{i}") for i in range(WIDE)]
        stored = [sem(f"stored{i}") for i in range(WIDE)]
        rows_written = sem("rows_written")
        d_row_loaded = sem("d_row_loaded")
        s_row_loaded = [sem(f"s_row_loaded{i}") for i in range(2)]
        const_step = sem("const_step")
        consts_ready = sem("consts_ready")
        bias_scaled = sem("bias_scaled")
        stats_raw = sem("stats_raw")
        stats_ready = sem("stats_ready")
        var_ready = sem("var_ready")
        rstd_ready = sem("rstd_ready")
        mean_rstd_ready = sem("mean_rstd_ready")
        shift_ready = sem("shift_ready")
        h_full_ready = sem("h_full_ready")
        h_hi_ready = sem("h_hi_ready")
        h_lo_ready = sem("h_lo_ready")
        prod_ready = sem("prod_ready")
        dot_ready = sem("dot_ready")
        rows_turned = sem("rows_turned")
        rows_ready = sem("rows_ready")
        d_min_ready = sem("d_min_ready")
        lift_raw_ready = sem("lift_raw_ready")
        lift_ready = sem("lift_ready")
        s_steep_ready = sem("s_steep_ready")
        d_steep_ready = sem("d_steep_ready")
        exp_bias_ready = sem("exp_bias_ready")
        adj_fixed = sem("adj_fixed")
        mask_ready = sem("mask_ready")
        part_ready = sem("part_ready")
        d_top_ready = sem("d_top_ready")
        d_max_ready = sem("d_max_ready")
        w_parts_ready = sem("w_parts_ready")
        w_sum_ready = sem("w_sum_ready")
        w_pos_ready = sem("w_pos_ready")
        w_max_ready = sem("w_max_ready")
        gate_ready = sem("gate_ready")
        gate_diag_ready = sem("gate_diag_ready")
        mask_turned = sem("mask_turned")
        score_ready = sem("score_ready")
        prob_ready = sem("prob_ready")
        prob_hi_ready = sem("prob_hi_ready")
        prob_lo_ready = sem("prob_lo_ready")
        unit_done = sem("unit_done")
        acc_ready = sem("acc_ready")
        inv_ready = sem("inv_ready")
        acc_read = [sem(f"acc_read{w}") for w in range(WIDE)]
        rest_ready = sem("rest_ready")
        rest_read = sem("rest_read")
        rest_added = sem("rest_added")
        x_added = [sem(f"x_added{w}") for w in range(WIDE)]

        def known_below(n, limit):
            return isinstance(n, int) and n < limit

        def batch_at(n):
            return Batch(n, STEPS * n, T * n, Q * n, N * n, n % 2, n == 0, n == B - 1)

        def over_batches(eng, body):
            with eng.Fori(0, B // 2 - 1) as pair:
                held = [eng.snap(pair * (2 * c)) for c in (1, STEPS, T, Q, N)]
                b0, b1, b2 = (Batch(*(h + c * k for h, c in zip(held, (1, STEPS, T, Q, N))), k % 2)
                              for k in range(3))
                body(b0, b1)
                body(b1, b2)
            body(batch_at(B - 2), batch_at(B - 1))
            body(batch_at(B - 1), None)

        first = batch_at(0)

        block = ctx.enter_context(nc.Block())

        def norm_products(eng, nb, t):
            n = nb.tiles + t
            eng.wait_ge(h_full_ready, n + 1)
            for v, w in enumerate((w_dst_b, w_src_b)):
                if not known_below(n, 1):
                    eng.wait_ge(dot_ready, 2 * n - 1 + v)
                eng.tensor_tensor(prod[:, v, :], h_full[:, t % 2, :], w[:, :], ALU.mult).then_inc(prod_ready, 1)

        def norm_low(eng, nb, t):
            eng.wait_ge(h_hi_ready, nb.tiles + t + 1)
            eng.tensor_tensor(h_lo[:, nb.slot, t, 0:H], h_full[:, t % 2, :], h_hi[:, nb.slot, t, 0:H],
                              ALU.subtract).then_inc(h_lo_ready, 1)

        @block.sync
        def _(sp):
            def load_x_norm(b, i):
                if not (b.first and i < 4):
                    sp.wait_ge(h_full_ready, b.tiles + i - 3)
                sp.dma_start(x_norm[:, i % 4, :], x_rows[bass.ds(b.rows + P * i, P), :]) \
                    .then_inc(x_norm_loaded[i % 4], 16)

            def load_adj(b, i):
                if not (b.first and i < 2):
                    sp.wait_ge(mask_ready, b.tiles + i - 1)
                sp.dma_start(adj_int[:, i % 2, :], adj_rows[bass.ds(b.rows + P * i, P), :]) \
                    .then_inc(adj_loaded[i % 2], 16)

            def wait_result(g, w):
                if w % 2 == 0:
                    sp.wait_ge(acc_read[w], g + 2)
                else:
                    sp.wait_ge(x_added[w], g + 1)
                sp.wait_ge(rest_added, g + 2)

            def load_x_res(b, q):
                for w in range(WIDE):
                    if not (b.first and q == 0):
                        wait_result(b.quarters + q - 1, w)
                    sp.dma_start(x_res[:, w, :], x_rows[bass.ds(b.rows + I * q + P * w, P), :]) \
                        .then_inc(x_res_loaded[w], 16)

            def store(b, q):
                for w in range(WIDE):
                    wait_result(b.quarters + q, w)
                    sp.dma_start(out_rows[bass.ds(b.rows + I * q + P * w, P), :], out_sb[:, w, :]) \
                        .then_inc(stored[w], 16)

            def write_rows(nb):
                sp.wait_ge(rows_ready, nb.index + 1)
                sp.dma_start(row_scratch[bass.ds(nb.index, 1), :].rearrange("a (r p) -> (a r) p", p=P), rows_sb[:, :]) \
                    .then_inc(rows_written, 16)

            def load_d_row(nb):
                sp.wait_ge(d_top_ready, nb.quarters)
                sp.wait_ge(rows_written, 16 * (nb.index + 1))
                sp.dma_start(d_row[:, :], row_scratch[bass.ds(nb.index, 1), 0:N].partition_broadcast(P)) \
                    .then_inc(d_row_loaded, 16)

            def load_s_row(b, q):
                if not (b.first and q == 0):
                    sp.wait_ge(score_ready, b.units + T * (q - 1) + 1)
                sp.wait_ge(rows_written, 16 * (b.index + 1))
                sp.dma_start(s_row[:, q % 2, :],
                             row_scratch[bass.ds(b.index, 1), N + I * q:N + I * (q + 1)].partition_broadcast(P)) \
                    .then_inc(s_row_loaded[q % 2], 16)

            sp.dma_start(w_src_b[:, :], w_src.rearrange("(a h) -> a h", a=1).partition_broadcast(P)) \
                .then_inc(weights_loaded, 16)
            sp.dma_start(w_dst_b[:, :], w_dst.rearrange("(a h) -> a h", a=1).partition_broadcast(P)) \
                .then_inc(weights_loaded, 16)
            sp.dma_start(bias_b[:, :], attn_b.rearrange("(a h) -> a h", a=1).partition_broadcast(P)) \
                .then_inc(weights_loaded, 16)
            for t in range(T):
                load_x_norm(first, t)
                if t == 4:
                    load_adj(first, 0)
                    load_adj(first, 1)
            load_adj(first, 2)
            load_adj(first, 3)
            write_rows(first)
            load_d_row(first)
            load_s_row(first, 0)
            for i in range(T, T + 4):
                load_x_norm(first, i)
            for i in range(WIDE, WIDE + 2):
                load_adj(first, i)
            load_x_res(first, 0)

            def steps(b, after):
                for s in range(STEPS):
                    q = s // T
                    for p in range(Q):
                        for k in range(WIDE):
                            i = WIDE * (p + 1) + k + 2
                            if s == MASK_STEP[p][k] and (i < T or after):
                                load_adj(b, i)
                    if s % T == 1 and q > 0:
                        store(b, q - 1)
                        load_x_res(b, q)
                    for t in range(T):
                        if s == NORM_STEP[t] + 2 and after and (t + 4 < T or not after.last):
                            load_x_norm(after, t + 4)
                    if s == ROWS_STEP and after:
                        write_rows(after)
                        load_d_row(after)
                    if s == q * T + 10 and q < Q - 1:
                        load_s_row(b, q + 1)
                    if s == (Q - 1) * T + 10 and after:
                        load_s_row(after, 0)
                store(b, Q - 1)
                if after:
                    load_x_res(after, 0)

            over_batches(sp, steps)
            for w in range(WIDE):
                sp.wait_ge(stored[w], 16 * (B * Q + 1))

        @block.gpsimd
        def _(pool):
            nc.gpsimd.memset(ident_f[:, :], 0.0).then_inc(const_step, 1)
            nc.gpsimd.memset(minus_half[:, :], -0.5).then_inc(consts_ready, 1)
            nc.gpsimd.memset(row_mul[:, :], STEEP).then_inc(const_step, 1)
            pool.wait_ge(const_step, 2)
            nc.gpsimd.memset(row_mul[0:T, :], ROW_SCALE).then_inc(consts_ready, 1)
            nc.gpsimd.affine_select(out=ident_f[:, :], in_=ident_f[:, :], compare_op=ALU.not_equal, fill=1.0,
                                    base=0, pattern=[[-1, P]], channel_multiplier=1).then_inc(const_step, 1)
            pool.wait_ge(const_step, 3)
            nc.gpsimd.tensor_copy(ident_b[:, :], ident_f[:, :]).then_inc(consts_ready, 1)
            nc.gpsimd.tensor_copy(ident_i[:, :], ident_f[:, :]).then_inc(consts_ready, 1)
            nc.gpsimd.memset(h_hi[:, :, :, H:HC], H_SCALE).then_inc(consts_ready, 1)
            pool.wait_ge(weights_loaded, 48)
            pool.nop(nofuse=True)
            nc.gpsimd.tensor_scalar(bias_steep[:, :], bias_b[:, :], STEEP, None, ALU.mult).then_inc(bias_scaled, 1)
            pool.wait_ge(bias_scaled, 1)
            nc.gpsimd.tensor_copy(row_add[:, :], bias_steep[0:2 * T, :]).then_inc(bias_scaled, 1)
            pool.wait_ge(bias_scaled, 2)
            nc.gpsimd.memset(row_add[0:T, :], 0.0).then_inc(consts_ready, 1)
            pool.wait_ge(consts_ready, 6)

            def norm_scalars(nb, t):
                n = nb.tiles + t
                pool.wait_ge(stats_ready, n + 1)
                pool.nop(nofuse=True)
                nc.gpsimd.tensor_scalar(var_eps[:, :], mean_var[:, t % 2, 1:2], EPS, H_SCALE ** -2,
                                        ALU.add, ALU.mult).then_inc(var_ready, 1)
                if not known_below(n, 2):
                    pool.wait_ge(h_full_ready, n - 1)
                pool.wait_ge(var_ready, n + 1)
                nc.gpsimd.tensor_tensor(rstd[:, t % 2:t % 2 + 1], var_eps[:, :], minus_half[:, :],
                                        ALU.pow).then_inc(rstd_ready, 1)
                pool.wait_ge(rstd_ready, n + 1)
                nc.gpsimd.tensor_tensor(mean_rstd[:, :], mean_var[:, t % 2, 0:1], rstd[:, t % 2:t % 2 + 1],
                                        ALU.mult).then_inc(mean_rstd_ready, 1)
                pool.wait_ge(mean_rstd_ready, n + 1)
                pool.nop(nofuse=True)
                nc.gpsimd.tensor_scalar(shift[:, t % 2:t % 2 + 1], mean_rstd[:, :], -1.0, None,
                                        ALU.mult).then_inc(shift_ready, 1)

            def batch_scalars(nb):
                pool.wait_ge(d_min_ready, nb.index + 1)
                pool.nop(nofuse=True)
                nc.gpsimd.tensor_scalar(lift_raw[:, :], d_min[:, :], -SLOPE / ROW_SCALE, 1.0,
                                        ALU.mult, ALU.add).then_inc(lift_raw_ready, 1)
                if not nb.first:
                    pool.wait_ge(gate_ready, nb.quarters)
                    pool.wait_ge(exp_bias_ready, nb.index)
                pool.wait_ge(lift_raw_ready, nb.index + 1)
                pool.nop(nofuse=True)
                nc.gpsimd.tensor_scalar(lift[:, :], lift_raw[:, :], 1.0, None, ALU.max).then_inc(lift_ready, 1)
                pool.wait_ge(dot_ready, 2 * nb.tiles + 2 * T)
                pool.nop(nofuse=True)
                nc.gpsimd.tensor_scalar(s_steep[:, :], dots[:, T:2 * T], STEEP, bias_steep[:, 0:1],
                                        ALU.mult, ALU.add).then_inc(s_steep_ready, 1)

            def fix_adj(nb, q, k):
                t = WIDE * q + k
                pool.wait_ge(adj_loaded[k % 2], 8 * nb.tiles + 16 * (t // 2 + 1))
                nc.gpsimd.tensor_tensor(adj_int[:, k % 2, t * P:(t + 1) * P], adj_int[:, k % 2, t * P:(t + 1) * P],
                                        ident_i[:, :], ALU.add).then_inc(adj_fixed, 1)

            def gates(nb, q):
                g = nb.quarters + q
                pool.wait_ge(d_top_ready, g + 1)
                pool.nop(nofuse=True)
                nc.gpsimd.tensor_scalar(d_max[:, :], d_top[:, :], TINY, 1.0 / ROW_SCALE,
                                        ALU.add, ALU.mult).then_inc(d_max_ready, 1)
                pool.wait_ge(d_max_ready, g + 1)
                pool.wait_ge(s_steep_ready, nb.index + 1)
                pool.nop(nofuse=True)
                nc.gpsimd.tensor_scalar(w_low[:, :], d_max[:, :], SLOPE, None, ALU.mult).then_inc(w_parts_ready, 1)
                nc.gpsimd.tensor_scalar(w_high[:, :], d_max[:, :], STEEP, None, ALU.mult).then_inc(w_parts_ready, 1)
                pool.wait_ge(w_parts_ready, 2 * (g + 1))
                nc.gpsimd.tensor_tensor(w_sum[:, :], w_high[:, :], s_steep[:, WIDE * q:WIDE * (q + 1)],
                                        ALU.add).then_inc(w_sum_ready, 1)
                pool.wait_ge(w_sum_ready, g + 1)
                pool.nop(nofuse=True)
                nc.gpsimd.tensor_scalar(w_pos[:, :], w_sum[:, :], 0.0, None, ALU.max).then_inc(w_pos_ready, 1)
                pool.wait_ge(w_pos_ready, g + 1)
                nc.gpsimd.tensor_tensor(w_max[:, :], w_low[:, :], w_pos[:, :], ALU.add).then_inc(w_max_ready, 1)
                pool.wait_ge(w_max_ready, g + 1)
                pool.wait_ge(lift_ready, nb.index + 1)
                pool.nop(nofuse=True)
                if not known_below(g, 1):
                    pool.wait_ge(gate_diag_ready, g)
                    pool.nop(nofuse=True)
                nc.gpsimd.tensor_scalar(gate[:, :], w_max[:, :], lift[:, 0:1], -1.0 / TINY,
                                        ALU.add, ALU.mult).then_inc(gate_ready, 1)

            def add_x(b, q, w):
                g = b.quarters + q
                pool.wait_ge(acc_read[w], g + 2)
                pool.wait_ge(x_res_loaded[w], 16 * g + 16)
                nc.gpsimd.tensor_tensor(out_sb[:, w, 0:MAIN], out_sb[:, w, 0:MAIN], x_res[:, w, 0:MAIN],
                                        ALU.add).then_inc(x_added[w], 1)

            for t in range(T):
                norm_scalars(first, t)
            for k in range(WIDE):
                fix_adj(first, 0, k)
            batch_scalars(first)
            gates(first, 0)

            def steps(b, after):
                for s in range(STEPS):
                    q = s // T
                    for p in range(Q):
                        nq, nb = (p + 1, b) if p < Q - 1 else (0, after)
                        if nb:
                            for k in range(WIDE):
                                if s == max(MASK_STEP[p][k] - 2, 0):
                                    fix_adj(nb, nq, k)
                            if s == GATE_STEP[p]:
                                gates(nb, nq)
                    if s % T == 0 and q > 0:
                        add_x(b, q - 1, 1)
                        add_x(b, q - 1, 3)
                    if after:
                        done = NORM_STEP.index(s - 2) if s - 2 in NORM_STEP else None
                        if done is not None:
                            norm_products(pool, after, done)
                        if s in NORM_STEP:
                            norm_scalars(after, NORM_STEP.index(s))
                        if done is not None:
                            norm_low(pool, after, done)
                        if s == D_MIN_STEP:
                            batch_scalars(after)
                add_x(b, Q - 1, 1)
                add_x(b, Q - 1, 3)

            over_batches(pool, steps)

        @block.scalar
        def _(act):
            def normalise(nb, t):
                n = nb.tiles + t
                act.wait_ge(x_norm_loaded[t % 4], 4 * nb.tiles + 16 * (t // 4 + 1))
                act.wait_ge(shift_ready, n + 1)
                if not known_below(n, 2):
                    act.wait_ge(h_lo_ready, n - 1)
                nc.scalar.activation(h_full[:, t % 2, :], x_norm[:, t % 4, :], ACT.Relu,
                                     bias=shift[:, t % 2:t % 2 + 1],
                                     scale=rstd[:, t % 2:t % 2 + 1]).then_inc(h_full_ready, 1)
                act.wait_ge(h_full_ready, n + 1)
                if not nb.first:
                    act.wait_ge(unit_done, nb.units - STEPS + 1)
                nc.scalar.activation(h_hi[:, nb.slot, t, 0:H], h_full[:, t % 2, :],
                                     ACT.Copy).then_inc(h_hi_ready, 1)

            def sum_products(nb, t):
                n = nb.tiles + t
                for v in range(2):
                    act.wait_ge(prod_ready, 2 * n + v + 1)
                    if t == 0 and v == 0 and not nb.first:
                        act.wait_ge(rows_turned, nb.index)
                        act.wait_ge(s_steep_ready, nb.index)
                        act.wait_ge(d_steep_ready, nb.index)
                        act.wait_ge(exp_bias_ready, nb.index)
                    nc.scalar.activation(prod_junk[:, v, :], prod[:, v, :], ACT.Copy, scale=1.0 / H_SCALE,
                                         accum_out=dots[:, v * T + t:v * T + t + 1]).then_inc(dot_ready, 1)

            def set_exp_bias(nb):
                if not nb.first:
                    act.wait_ge(prob_ready, nb.units)
                act.wait_ge(lift_ready, nb.index + 1)
                act.wait_ge(dot_ready, 2 * nb.tiles + 2 * T)
                nc.scalar.activation(exp_bias[:, :], dots[:, 0:T], ACT.Identity,
                                     bias=lift[:, 0:1]).then_inc(exp_bias_ready, 1)

            def probabilities(b, s):
                u = b.units + s
                j = s % T
                act.wait_ge(score_ready, u + 1)
                if s == 0:
                    act.wait_ge(exp_bias_ready, b.index + 1)
                nc.scalar.activation(prob[:, s % 2, :], score[:, s % 2, :], ACT.Exp,
                                     bias=exp_bias[:, j:j + 1]).then_inc(prob_ready, 1)
                act.wait_ge(prob_ready, u + 1)
                nc.scalar.activation(prob_hi[:, s % 4, :], prob[:, s % 2, :], ACT.Copy,
                                     scale=P_SCALE).then_inc(prob_hi_ready, 1)

            def scale_result(b, q, w):
                g = b.quarters + q
                act.wait_ge(inv_ready, g + 1)
                act.wait_ge(stored[w], 16 * g + 16)
                if w < WIDE - 1:
                    act.wait_ge(acc_ready, (WIDE - 1) * g + w + 1)
                else:
                    act.wait_ge(unit_done, b.units + T * (q + 1))
                nc.scalar.activation(out_sb[:, w, 0:MAIN], acc[:, w, 0:MAIN], ACT.Copy,
                                     scale=inv_sum[:, w:w + 1]).then_inc(acc_read[w], 1)

            for t in range(T + 1):
                if t < T:
                    normalise(first, t)
                if t > 0:
                    sum_products(first, t - 1)
            set_exp_bias(first)
            for s in range(AHEAD):
                probabilities(first, s)

            def steps(b, after):
                for s in range(STEPS):
                    a = s + AHEAD
                    if a == STEPS and after:
                        set_exp_bias(after)
                    if s % T == T - 1:
                        scale_result(b, s // T, 1)
                    if a < STEPS or after:
                        probabilities(b if a < STEPS else after, a % STEPS)
                    if after:
                        for t in range(T):
                            if s == NORM_STEP[t] + 2:
                                normalise(after, t)
                            if s == SUM_STEP[t]:
                                sum_products(after, t)
                    if s % T == T - 1:
                        scale_result(b, s // T, 3)

            over_batches(act, steps)

        @block.vector
        def _(dve):
            def norm_stats(nb, t):
                n = nb.tiles + t
                dve.wait_ge(x_norm_loaded[t % 4], 4 * nb.tiles + 16 * (t // 4 + 1))
                nc.vector.bn_stats(stats[:, t % 2, :], x_norm[:, t % 4, :]).then_inc(stats_raw, 1)

            def norm_mean_var(nb, t):
                n = nb.tiles + t
                dve.wait_ge(stats_raw, n + 1)
                if not known_below(n, 2):
                    dve.wait_ge(shift_ready, n - 1)
                dve.nop(nofuse=True)
                nc.vector.bn_aggr(mean_var[:, t % 2, :], stats[:, t % 2, :]).then_inc(stats_ready, 1)

            def take_rows(nb):
                dve.wait_ge(consts_ready, 6)
                dve.wait_ge(rows_turned, nb.index + 1)
                if not nb.first:
                    dve.wait_ge(rows_written, 16 * nb.index)
                nc.vector.tensor_scalar(rows_sb[:, :], rows_ps[0:2 * T, 0:P], row_mul[:, 0:1], row_add[:, 0:1],
                                        ALU.mult, ALU.add).then_inc(rows_ready, 1)

            def take_d_min(nb):
                dve.wait_ge(d_row_loaded, 16 * (nb.index + 1))
                if not nb.first:
                    dve.wait_ge(lift_raw_ready, nb.index)
                nc.vector.tensor_reduce(d_min[:, :], d_row[:, :], AX.X, ALU.min).then_inc(d_min_ready, 1)

            def make_mask(nb, q, k):
                g = nb.quarters + q
                dve.wait_ge(adj_fixed, nb.tiles + WIDE * q + k + 1)
                if not known_below(g, 2):
                    dve.wait_ge(mask_turned, T * (g - 1) + 1)
                nc.vector.tensor_scalar(mask[:, q % 2, k, :], adj_int[:, k % 2, :], 0.0, TINY,
                                        ALU.is_equal, ALU.max).then_inc(mask_ready, 1)

            def search_mask(nb, q, k, h):
                n = nb.tiles + WIDE * q + k
                g = nb.quarters + q
                cols = slice(h * N // HALVES, (h + 1) * N // HALVES)
                if h == 0:
                    dve.wait_ge(mask_ready, n + 1)
                    dve.wait_ge(d_row_loaded, 16 * (nb.index + 1))
                if not known_below(n, 1):
                    dve.wait_ge(part_ready, HALVES * n)
                if k == 0 and not known_below(g, 1):
                    dve.wait_ge(d_top_ready, g)
                dve.nop(nofuse=True)
                nc.vector.tensor_tensor_reduce(max_junk[:, cols], d_row[:, cols], mask[:, q % 2, k, cols], 1.0,
                                               LOWEST, ALU.subtract, ALU.max,
                                               d_part[:, h, k:k + 1]).then_inc(part_ready, 1)

            def join_parts(nb, q):
                g = nb.quarters + q
                dve.wait_ge(part_ready, HALVES * WIDE * (g + 1))
                if not known_below(g, 1):
                    dve.wait_ge(d_max_ready, g)
                nc.vector.tensor_tensor(d_top[:, :], d_part[:, 0, :], d_part[:, 1, :],
                                        ALU.max).then_inc(d_top_ready, 1)

            def set_d_steep(nb):
                if not nb.first:
                    dve.wait_ge(score_ready, nb.units)
                dve.wait_ge(dot_ready, 2 * nb.tiles + 2 * T)
                nc.vector.tensor_scalar(d_steep[:, :], dots[:, 0:T], -STEEP, None,
                                        ALU.mult).then_inc(d_steep_ready, 1)

            def scores(b, s):
                u = b.units + s
                q, j = s // T, s % T
                if s == 0:
                    dve.wait_ge(d_steep_ready, b.index + 1)
                if j == 0:
                    dve.wait_ge(s_row_loaded[q % 2], 8 * b.quarters + 16 * (q // 2 + 1))
                dve.wait_ge(mask_turned, u + 1)
                nc.vector.scalar_tensor_tensor(score[:, s % 2, :], s_row[:, q % 2, :], d_steep[:, j:j + 1],
                                               gate_ps[s % 2][:, 0:I], ALU.max, ALU.add).then_inc(score_ready, 1)

            def low_halves(b, s):
                u = b.units + s
                dve.wait_ge(prob_hi_ready, u + 1)
                nc.vector.scalar_tensor_tensor(prob_lo[:, s % 4, :], prob[:, s % 2, :], P_SCALE,
                                               prob_hi[:, s % 4, :], ALU.mult,
                                               ALU.subtract).then_inc(prob_lo_ready, 1)

            def take_rest(b, q):
                g = b.quarters + q
                dve.wait_ge(rest_ready, g + 1)
                dve.wait_ge(rest_added, g + 1)
                for w in range(1, WIDE, 2):
                    dve.wait_ge(acc_read[w], g + 1)
                columns = acc_rest[:, 0:WIDE * (REST + 1)].rearrange("p (w c) -> p w c", w=WIDE)
                nc.vector.reciprocal(inv_sum[:, :], columns[:, :, REST]).then_inc(inv_ready, 1)
                nc.vector.tensor_copy(rest_sb[:, :, :], columns[:, :, 0:REST]).then_inc(rest_read, 1)

            def finish(b, q, w):
                g = b.quarters + q
                dve.wait_ge(acc_ready, (WIDE - 1) * g + w + 1)
                dve.wait_ge(inv_ready, g + 1)
                dve.wait_ge(x_res_loaded[w], 16 * g + 16)
                dve.wait_ge(stored[w], 16 * g + 16)
                nc.vector.scalar_tensor_tensor(out_sb[:, w, 0:MAIN], acc[:, w, 0:MAIN], inv_sum[:, w:w + 1],
                                               x_res[:, w, 0:MAIN], ALU.mult, ALU.add).then_inc(acc_read[w], 1)

            def finish_rest(b, q):
                g = b.quarters + q
                dve.wait_ge(rest_read, g + 2)
                for w in range(WIDE):
                    if w % 2:
                        dve.wait_ge(x_res_loaded[w], 16 * g + 16)
                        dve.wait_ge(stored[w], 16 * g + 16)
                    last = nc.vector.scalar_tensor_tensor(out_sb[:, w, MAIN:H], rest_sb[:, w, 0:REST],
                                                          inv_sum[:, w:w + 1], x_res[:, w, MAIN:H],
                                                          ALU.mult, ALU.add)
                last.then_inc(rest_added, 1)

            def diagonals(nb, q):
                g = nb.quarters + q
                dve.wait_ge(gate_ready, g + 1)
                if not known_below(g, 2):
                    dve.wait_ge(mask_turned, T * (g - 1) + 1)
                for k in range(WIDE):
                    last = nc.vector.tensor_scalar(gate_diag[:, q % 2, k, :], ident_b[:, :], gate[:, k:k + 1],
                                                   None, ALU.mult)
                last.then_inc(gate_diag_ready, 1)

            dve.sem_inc(rest_read, 1)
            dve.sem_inc(rest_added, 1)
            for w in range(WIDE):
                dve.sem_inc(acc_read[w], 1)
                dve.sem_inc(stored[w], 16)
            dve.wait_ge(weights_loaded, 48)
            for t in range(T + 2):
                if t < T:
                    norm_stats(first, t)
                    norm_mean_var(first, t)
                if t > 1:
                    norm_products(dve, first, t - 2)
                    norm_low(dve, first, t - 2)
            take_rows(first)
            set_d_steep(first)
            for k in range(WIDE):
                make_mask(first, 0, k)
            take_d_min(first)
            for k in range(WIDE):
                for h in range(HALVES):
                    search_mask(first, 0, k, h)
            join_parts(first, 0)
            diagonals(first, 0)
            scores(first, 0)
            scores(first, 1)
            low_halves(first, 0)

            def steps(b, after):
                for s in range(STEPS):
                    q = s // T
                    a = s + AHEAD
                    if a == STEPS and after:
                        set_d_steep(after)
                    if a < STEPS or after:
                        scores(b if a < STEPS else after, a % STEPS)
                    if s % T == T - 1:
                        take_rest(b, q)
                    if a - 1 < STEPS or after:
                        low_halves(b if a - 1 < STEPS else after, (a - 1) % STEPS)
                    if s % T == T - 1:
                        finish(b, q, 0)
                        finish(b, q, 2)
                    if s % T == 0 and q > 0:
                        finish_rest(b, q - 1)
                    if after:
                        for t in range(T):
                            if s == NORM_STEP[t]:
                                norm_stats(after, t)
                        if s == ROWS_STEP:
                            take_rows(after)
                        if s == D_MIN_STEP:
                            take_d_min(after)
                    for p in range(Q):
                        nq, nb = (p + 1, b) if p < Q - 1 else (0, after)
                        if nb:
                            for k in range(WIDE):
                                if s == MASK_STEP[p][k]:
                                    make_mask(nb, nq, k)
                                for h in range(HALVES):
                                    if s == TOP_STEP[p][k][h]:
                                        search_mask(nb, nq, k, h)
                            if s == GATE_STEP[p]:
                                join_parts(nb, nq)
                            if s == GATE_STEP[p] + 2:
                                diagonals(nb, nq)
                    if after:
                        for t in range(T):
                            if s == NORM_STEP[t]:
                                norm_mean_var(after, t)
                finish_rest(b, Q - 1)

            over_batches(dve, steps)

        @block.tensor
        def _(pe):
            def turn_rows(nb):
                pe.wait_ge(dot_ready, 2 * nb.tiles + 2 * T)
                if not nb.first:
                    pe.wait_ge(rows_ready, nb.index)
                nc.tensor.transpose(rows_ps[0:2 * T, 0:P], dots[:, :], ident_f[:, :]).then_inc(rows_turned, 1)

            def turn_masks(b, s):
                u = b.units + s
                q, j = s // T, s % T
                if j == 0:
                    pe.wait_ge(gate_diag_ready, b.quarters + q + 1)
                    pe.wait_ge(mask_ready, b.tiles + WIDE * (q + 1))
                for k in range(WIDE):
                    last = nc.tensor.matmul(gate_ps[s % 2][:, k * P:(k + 1) * P],
                                            mask[:, q % 2, k, j * P:(j + 1) * P], gate_diag[:, q % 2, k, :],
                                            start=True, stop=True)
                last.then_inc(mask_turned, 1)

            def multiply(b, s):
                u = b.units + s
                q, j = s // T, s % T
                if s == 0:
                    pe.wait_ge(h_lo_ready, b.tiles + T)
                hi = h_hi[:, b.slot, j, :]
                lo = h_lo[:, b.slot, j, :]
                start, stop = j == 0, j == T - 1
                if start:
                    pe.wait_ge(rest_read, b.quarters + q + 1)
                for w in range(WIDE):
                    p_hi = prob_hi[:, s % 4, w * P:(w + 1) * P]
                    p_lo = prob_lo[:, s % 4, w * P:(w + 1) * P]
                    c = w * (REST + 1)
                    rest = acc_rest[:, c:c + REST + 1]
                    nc.tensor.matmul(rest, p_hi, hi[:, MAIN:H + 1], start=start and w == 0, stop=False,
                                     skip_group_check=True)
                    nc.tensor.matmul(acc_rest[:, c:c + REST], p_hi, lo[:, MAIN:H], start=False, stop=False,
                                     skip_group_check=True)
                    last = nc.tensor.matmul(rest, p_lo, hi[:, MAIN:H + 1], start=False, stop=stop,
                                            skip_group_check=True)
                if stop:
                    last.then_inc(rest_ready, 1)
                for w in range(WIDE):
                    if start:
                        pe.wait_ge(acc_read[w], b.quarters + q + 1)
                    p_hi = prob_hi[:, s % 4, w * P:(w + 1) * P]
                    p_lo = prob_lo[:, s % 4, w * P:(w + 1) * P]
                    main = acc[:, w, 0:MAIN]
                    nc.tensor.matmul(main, p_hi, hi[:, 0:MAIN], start=start, stop=False)
                    nc.tensor.matmul(main, p_hi, lo[:, 0:MAIN], start=False, stop=False)
                    last = nc.tensor.matmul(main, p_lo, hi[:, 0:MAIN], start=False, stop=stop)
                    if stop and w < WIDE - 1:
                        last.then_inc(acc_ready, 1)
                last.then_inc(unit_done, 1)

            pe.wait_ge(consts_ready, 6)
            turn_rows(first)
            turn_masks(first, 0)
            turn_masks(first, 1)

            def steps(b, after):
                for s in range(STEPS):
                    a = s + AHEAD
                    if s == ROWS_STEP and after:
                        turn_rows(after)
                    pe.wait_ge(prob_lo_ready, b.units + s + 1)
                    if a < STEPS or after:
                        turn_masks(b if a < STEPS else after, a % STEPS)
                    multiply(b, s)

            over_batches(pe, steps)


_INS = ["x", "adj", "L0_gnn_attn_w_src", "L0_gnn_attn_w_dst", "L0_gnn_attn_b"]


def kernel(**inputs):
    import numpy as _np
    import concourse.bacc as _bacc
    from concourse import mybir as _mybir
    from concourse.bass_utils import run_bass_kernel_spmd as _run

    nc = _bacc.Bacc("TRN2", target_bir_lowering=False, num_devices=1)
    arrays, args = {}, []
    for name in _INS:
        a = _np.ascontiguousarray(inputs[name])
        arrays[f"in_{name}_dram"] = a
        args.append(nc.dram_tensor(f"in_{name}_dram", a.shape, _mybir.dt.from_np(a.dtype), kind="ExternalInput").ap())
    x = arrays["in_x_dram"]
    args.append(nc.dram_tensor("out_0_dram", x.shape, _mybir.dt.from_np(x.dtype), kind="ExternalOutput").ap())
    gnn_layer(nc, *args)
    r = _run(nc, [arrays], core_ids=[0])
    return r.results[0]["out_0_dram"]
```

```python
from contextlib import ExitStack

import concourse.bass as bass
from concourse import mybir

F32 = mybir.dt.float32
F16 = mybir.dt.float16
BF16 = mybir.dt.bfloat16
I32 = mybir.dt.int32
ALU = mybir.AluOpType
ACT = mybir.ActivationFunctionType
AX = mybir.AxisListType

P = 128
SLOPE = 0.2
STEEP = 1.0 - SLOPE
EPS = 1e-5
P_SCALE = 4096.0
H_SCALE = 512.0
TINY = 2.0 ** -60
ROW_SCALE = 2.0 ** -65
LOWEST = -3.0e38


class Batch:

    def __init__(self, index, units, tiles, quarters, rows, slot, first=False, last=False):
        self.index, self.units, self.tiles, self.quarters, self.rows = index, units, tiles, quarters, rows
        self.slot = slot
        self.first = first
        self.last = last


def gnn_layer(nc, x, adj, w_src, w_dst, attn_b, out):
    B, N, H = x.shape
    T = N // P
    WIDE = 4
    Q = T // WIDE
    I = WIDE * P
    STEPS = Q * T
    MAIN = 460
    REST = H - MAIN
    HC = H + 2
    AHEAD = 2

    x_rows = x.rearrange("b n h -> (b n) h")
    adj_rows = adj.rearrange("b i j -> (b i) j")
    out_rows = out.rearrange("b n h -> (b n) h")
    row_scratch = nc.dram_tensor("row_scratch", [B, 2 * T * P], F32, kind="Internal").ap()

    HALVES = 2
    PER_QUARTER = 6
    NORM_STEP = [T * (t // PER_QUARTER) + 1 + 2 * (t % PER_QUARTER) for t in range(T)]
    SUM_STEP = [s + 3 if s % T < T - 5 else s + 5 for s in NORM_STEP]
    ROWS_STEP = SUM_STEP[-1] + 2
    D_MIN_STEP = ROWS_STEP + 2
    MASK_STEP = [[q * T + 3 * k for k in range(WIDE)] for q in range(Q)]
    TOP_STEP = [[[s + 1 + h for h in range(HALVES)] for s in MASK_STEP[q]] for q in range(Q)]
    MASK_STEP[Q - 1][0] = (Q - 1) * T - 2
    GATE_STEP = [TOP_STEP[q][WIDE - 1][HALVES - 1] for q in range(Q)]

    FIRST_MASK = [8, 10, 13, 15]
    FIRST_LOAD = [4, 6, 12, 14]

    nc.disable_value_cache = True
    with ExitStack() as ctx:
        def sb(name, shape, dt):
            return ctx.enter_context(nc.sbuf_tensor(name, shape, dt))

        def ps(name, shape, dt):
            return ctx.enter_context(nc.psum_tensor(name, shape, dt))

        def sem(name):
            return ctx.enter_context(nc.semaphore(name))

        adj_int = sb("adj_int", [P, 2, N], I32)
        mask = sb("mask", [P, 2, WIDE, N], BF16)
        gate_diag = sb("gate_diag", [P, 2, WIDE, P], BF16)
        h_hi = sb("h_hi", [P, 2, T, HC], F16)
        h_lo = sb("h_lo", [P, 2, T, HC], F16)
        x_norm = sb("x_norm", [P, 4, H], F32)
        x_res = sb("x_res", [P, WIDE, H], F32)
        out_sb = sb("out_sb", [P, WIDE, H], F32)
        h_full = sb("h_full", [P, 2, H], F32)
        prod = sb("prod", [P, 2, H], F32)
        prod_junk = sb("prod_junk", [P, 2, H], BF16)
        max_junk = sb("max_junk", [P, N], BF16)
        score = sb("score", [P, 2, I], F32)
        prob = sb("prob", [P, 2, I], F32)
        prob_hi = sb("prob_hi", [P, 4, I], F16)
        prob_lo = sb("prob_lo", [P, 4, I], F16)
        d_row = sb("d_row", [P, N], F32)
        s_row = sb("s_row", [P, 2, I], F32)
        w_src_b = sb("w_src_b", [P, H], F32)
        w_dst_b = sb("w_dst_b", [P, H], F32)
        bias_b = sb("bias_b", [P, 1], F32)
        bias_steep = sb("bias_steep", [P, 1], F32)
        ident_f = sb("ident_f", [P, P], F32)
        ident_b = sb("ident_b", [P, P], BF16)
        ones_f = sb("ones_f", [P, P], F32)
        d_diag = sb("d_diag", [P, 2, P], F32)
        ident_i = sb("ident_i", [P, P], I32)
        stats = sb("stats", [P, 2, 6], F32)
        mean_var = sb("mean_var", [P, 2, 2], F32)
        var_eps = sb("var_eps", [P, 1], F32)
        minus_half = sb("minus_half", [P, 1], F32)
        rstd = sb("rstd", [P, 2], F32)
        shift = sb("shift", [P, 2], F32)
        dots = sb("dots", [P, 2 * T], F32)
        d_steep = sb("d_steep", [P, T], F32)
        s_steep = sb("s_steep", [P, T], F32)
        exp_bias = sb("exp_bias", [P, T], F32)
        d_low = sb("d_low", [P, 1], F32)
        d_low_diag = sb("d_low_diag", [P, P], F32)
        d_min = sb("d_min", [P, 1], F32)
        lift_raw = sb("lift_raw", [P, 1], F32)
        lift = sb("lift", [P, 1], F32)
        rows_sb = sb("rows_sb", [2 * T, P], F32)
        row_mul = sb("row_mul", [2 * T, 1], F32)
        row_add = sb("row_add", [2 * T, 1], F32)
        d_part = sb("d_part", [P, HALVES, WIDE], F32)
        d_top = sb("d_top", [P, WIDE], F32)
        d_max = sb("d_max", [P, WIDE], F32)
        w_low = sb("w_low", [P, WIDE], F32)
        w_high = sb("w_high", [P, WIDE], F32)
        w_sum = sb("w_sum", [P, WIDE], F32)
        w_pos = sb("w_pos", [P, WIDE], F32)
        w_max = sb("w_max", [P, WIDE], F32)
        gate = sb("gate", [P, WIDE], F32)
        rest_sb = sb("rest_sb", [P, WIDE, REST], F32)
        inv_sum = sb("inv_sum", [P, WIDE], F32)

        acc = ps("acc", [P, WIDE, 512], F32)
        acc_rest = ps("acc_rest", [P, 512], F32)
        gate_ps = [ps(f"gate_ps{i}", [P, 512], F32) for i in range(2)]
        rows_ps = ps("rows_ps", [P, 512], F32)

        weights_loaded = sem("weights_loaded")
        adj_loaded = [sem(f"adj_loaded{i}") for i in range(2)]
        x_norm_loaded = [sem(f"x_norm_loaded{i}") for i in range(4)]
        x_res_loaded = [sem(f"x_res_loaded{i}") for i in range(WIDE)]
        stored = [sem(f"stored{i}") for i in range(WIDE)]
        rows_written = sem("rows_written")
        d_row_ready = sem("d_row_ready")
        s_row_loaded = [sem(f"s_row_loaded{i}") for i in range(2)]
        const_step = sem("const_step")
        consts_ready = sem("consts_ready")
        bias_scaled = sem("bias_scaled")
        stats_raw = sem("stats_raw")
        stats_ready = sem("stats_ready")
        var_ready = sem("var_ready")
        rstd_ready = sem("rstd_ready")
        shift_ready = sem("shift_ready")
        h_full_ready = sem("h_full_ready")
        h_hi_ready = sem("h_hi_ready")
        h_lo_ready = sem("h_lo_ready")
        prod_ready = sem("prod_ready")
        dot_ready = sem("dot_ready")
        d_diag_ready = sem("d_diag_ready")
        d_spread = sem("d_spread")
        rows_turned = sem("rows_turned")
        rows_ready = sem("rows_ready")
        d_low_ready = sem("d_low_ready")
        d_low_diag_ready = sem("d_low_diag_ready")
        d_low_spread = sem("d_low_spread")
        d_min_ready = sem("d_min_ready")
        lift_raw_ready = sem("lift_raw_ready")
        lift_ready = sem("lift_ready")
        s_steep_ready = sem("s_steep_ready")
        d_steep_ready = sem("d_steep_ready")
        exp_bias_ready = sem("exp_bias_ready")
        adj_fixed = sem("adj_fixed")
        mask_ready = sem("mask_ready")
        part_ready = sem("part_ready")
        d_top_ready = sem("d_top_ready")
        d_max_ready = sem("d_max_ready")
        w_parts_ready = sem("w_parts_ready")
        w_sum_ready = sem("w_sum_ready")
        w_pos_ready = sem("w_pos_ready")
        w_max_ready = sem("w_max_ready")
        gate_ready = sem("gate_ready")
        gate_diag_ready = sem("gate_diag_ready")
        mask_turned = sem("mask_turned")
        score_ready = sem("score_ready")
        prob_ready = sem("prob_ready")
        prob_hi_ready = sem("prob_hi_ready")
        prob_lo_ready = sem("prob_lo_ready")
        unit_done = sem("unit_done")
        acc_ready = sem("acc_ready")
        inv_ready = sem("inv_ready")
        acc_read = [sem(f"acc_read{w}") for w in range(WIDE)]
        rest_ready = sem("rest_ready")
        rest_read = sem("rest_read")
        rest_added = sem("rest_added")
        x_added = [sem(f"x_added{w}") for w in range(WIDE)]

        def known_below(n, limit):
            return isinstance(n, int) and n < limit

        def batch_at(n):
            return Batch(n, STEPS * n, T * n, Q * n, N * n, n % 2, n == 0, n == B - 1)

        def over_batches(eng, body):
            with eng.Fori(0, B // 2 - 1) as pair:
                held = [eng.snap(pair * (2 * c)) for c in (1, STEPS, T, Q, N)]
                b0, b1, b2 = (Batch(*(h + c * k for h, c in zip(held, (1, STEPS, T, Q, N))), k % 2)
                              for k in range(3))
                body(b0, b1)
                body(b1, b2)
            body(batch_at(B - 2), batch_at(B - 1))
            body(batch_at(B - 1), None)

        first = batch_at(0)

        block = ctx.enter_context(nc.Block())

        @block.sync
        def _(sp):
            def load_x_norm(b, i):
                if not (b.first and i < 4):
                    sp.wait_ge(h_full_ready, b.tiles + i - 3)
                sp.dma_start(x_norm[:, i % 4, :], x_rows[bass.ds(b.rows + P * i, P), :]) \
                    .then_inc(x_norm_loaded[i % 4], 16)

            def load_adj(b, i):
                if not (b.first and i < 2):
                    sp.wait_ge(mask_ready, b.tiles + i - 1)
                sp.dma_start(adj_int[:, i % 2, :], adj_rows[bass.ds(b.rows + P * i, P), :]) \
                    .then_inc(adj_loaded[i % 2], 16)

            def wait_result(g, w):
                if w % 2 == 0:
                    sp.wait_ge(acc_read[w], g + 2)
                else:
                    sp.wait_ge(x_added[w], g + 1)
                sp.wait_ge(rest_added, g + 2)

            def load_x_res(b, q):
                for w in range(WIDE):
                    if not (b.first and q == 0):
                        wait_result(b.quarters + q - 1, w)
                    sp.dma_start(x_res[:, w, :], x_rows[bass.ds(b.rows + I * q + P * w, P), :]) \
                        .then_inc(x_res_loaded[w], 16)

            def store(b, q):
                for w in range(WIDE):
                    wait_result(b.quarters + q, w)
                    sp.dma_start(out_rows[bass.ds(b.rows + I * q + P * w, P), :], out_sb[:, w, :]) \
                        .then_inc(stored[w], 16)

            def write_rows(nb):
                sp.wait_ge(rows_ready, nb.index + 1)
                sp.dma_start(row_scratch[bass.ds(nb.index, 1), :].rearrange("a (r p) -> (a r) p", p=P), rows_sb[:, :]) \
                    .then_inc(rows_written, 16)

            def load_d_row(nb):
                sp.wait_ge(d_top_ready, nb.quarters)
                sp.wait_ge(rows_written, 16 * (nb.index + 1))
                sp.dma_start(d_row[:, :], row_scratch[bass.ds(nb.index, 1), 0:N].partition_broadcast(P)) \
                    .then_inc(d_row_ready, 16)

            def load_s_row(b, q):
                if not (b.first and q == 0):
                    sp.wait_ge(score_ready, b.units + T * (q - 1) + 1)
                sp.wait_ge(rows_written, 16 * (b.index + 1))
                sp.dma_start(s_row[:, q % 2, :],
                             row_scratch[bass.ds(b.index, 1), N + I * q:N + I * (q + 1)].partition_broadcast(P)) \
                    .then_inc(s_row_loaded[q % 2], 16)

            for t in range(T):
                load_x_norm(first, t)
                if t == 1:
                    sp.dma_start(w_src_b[:, :], w_src.rearrange("(a h) -> a h", a=1).partition_broadcast(P)) \
                        .then_inc(weights_loaded, 16)
                    sp.dma_start(w_dst_b[:, :], w_dst.rearrange("(a h) -> a h", a=1).partition_broadcast(P)) \
                        .then_inc(weights_loaded, 16)
                    sp.dma_start(bias_b[:, :], attn_b.rearrange("(a h) -> a h", a=1).partition_broadcast(P)) \
                        .then_inc(weights_loaded, 16)
                for k in range(WIDE):
                    if t == FIRST_LOAD[k]:
                        load_adj(first, k)
            write_rows(first)
            load_s_row(first, 0)
            for i in range(T, T + 4):
                load_x_norm(first, i)
            for i in range(WIDE, WIDE + 2):
                load_adj(first, i)
            load_x_res(first, 0)

            def steps(b, after):
                for s in range(STEPS):
                    q = s // T
                    for p in range(Q):
                        for k in range(WIDE):
                            i = WIDE * (p + 1) + k + 2
                            if s == MASK_STEP[p][k] and (i < T or after):
                                load_adj(b, i)
                    if s % T == 1 and q > 0:
                        store(b, q - 1)
                        load_x_res(b, q)
                    for t in range(T):
                        if s == NORM_STEP[t] + 2 and after and (t + 4 < T or not after.last):
                            load_x_norm(after, t + 4)
                    if s == ROWS_STEP and after:
                        write_rows(after)
                        load_d_row(after)
                    if s == q * T + 10 and q < Q - 1:
                        load_s_row(b, q + 1)
                    if s == (Q - 1) * T + 10 and after:
                        load_s_row(after, 0)
                store(b, Q - 1)
                if after:
                    load_x_res(after, 0)

            over_batches(sp, steps)
            for w in range(WIDE):
                sp.wait_ge(stored[w], 16 * (B * Q + 1))

        @block.gpsimd
        def _(pool):
            nc.gpsimd.memset(ident_f[:, :], 0.0).then_inc(const_step, 1)
            nc.gpsimd.memset(minus_half[:, :], -0.5).then_inc(consts_ready, 1)
            nc.gpsimd.memset(row_mul[:, :], STEEP).then_inc(const_step, 1)
            pool.wait_ge(const_step, 2)
            nc.gpsimd.memset(row_mul[0:T, :], ROW_SCALE).then_inc(consts_ready, 1)
            nc.gpsimd.affine_select(out=ident_f[:, :], in_=ident_f[:, :], compare_op=ALU.not_equal, fill=1.0,
                                    base=0, pattern=[[-1, P]], channel_multiplier=1).then_inc(const_step, 1)
            pool.wait_ge(const_step, 3)
            nc.gpsimd.tensor_copy(ident_b[:, :], ident_f[:, :]).then_inc(consts_ready, 1)
            nc.gpsimd.tensor_copy(ident_i[:, :], ident_f[:, :]).then_inc(consts_ready, 1)
            nc.gpsimd.memset(h_hi[:, :, :, H:HC], H_SCALE).then_inc(consts_ready, 1)
            nc.gpsimd.memset(ones_f[:, :], 1.0).then_inc(consts_ready, 1)
            pool.wait_ge(bias_scaled, 1)
            nc.gpsimd.tensor_copy(row_add[:, :], bias_steep[0:2 * T, :]).then_inc(bias_scaled, 1)
            pool.wait_ge(bias_scaled, 2)
            nc.gpsimd.memset(row_add[0:T, :], 0.0).then_inc(consts_ready, 1)
            pool.wait_ge(consts_ready, 7)

            def norm_scalars(nb, t):
                n = nb.tiles + t
                pool.wait_ge(stats_ready, n + 1)
                pool.nop(nofuse=True)
                nc.gpsimd.tensor_scalar(var_eps[:, :], mean_var[:, t % 2, 1:2], EPS, H_SCALE ** -2,
                                        ALU.add, ALU.mult).then_inc(var_ready, 1)
                if not known_below(n, 2):
                    pool.wait_ge(h_full_ready, n - 1)
                pool.wait_ge(var_ready, n + 1)
                nc.gpsimd.tensor_tensor(rstd[:, t % 2:t % 2 + 1], var_eps[:, :], minus_half[:, :],
                                        ALU.pow).then_inc(rstd_ready, 1)
                pool.wait_ge(rstd_ready, n + 1)
                pool.nop(nofuse=True)
                nc.gpsimd.tensor_scalar(shift[:, t % 2:t % 2 + 1], mean_var[:, t % 2, 0:1], rstd[:, t % 2:t % 2 + 1],
                                        -1.0, ALU.mult, ALU.mult).then_inc(shift_ready, 1)

            def norm_products(nb, t):
                n = nb.tiles + t
                pool.wait_ge(h_full_ready, n + 1)
                for v, w in enumerate((w_dst_b, w_src_b)):
                    pool.wait_ge(dot_ready, 2 * n - 1 + v)
                    nc.gpsimd.tensor_tensor(prod[:, v, :], h_full[:, t % 2, :], w[:, :],
                                            ALU.mult).then_inc(prod_ready, 1)

            def norm_low(nb, t):
                pool.wait_ge(h_hi_ready, nb.tiles + t + 1)
                nc.gpsimd.tensor_tensor(h_lo[:, nb.slot, t, 0:H], h_full[:, t % 2, :], h_hi[:, nb.slot, t, 0:H],
                                        ALU.subtract).then_inc(h_lo_ready, 1)

            def d_low_diagonal(nb):
                pool.wait_ge(d_low_ready, nb.index + 1)
                if not nb.first:
                    pool.wait_ge(d_low_spread, nb.index)
                pool.nop(nofuse=True)
                nc.gpsimd.tensor_scalar(d_low_diag[:, :], ident_f[:, :], d_low[:, 0:1], None,
                                        ALU.mult).then_inc(d_low_diag_ready, 1)

            def batch_scalars(nb):
                pool.wait_ge(d_min_ready, nb.index + 1)
                pool.nop(nofuse=True)
                nc.gpsimd.tensor_scalar(lift_raw[:, :], d_min[:, :], -SLOPE, 1.0,
                                        ALU.mult, ALU.add).then_inc(lift_raw_ready, 1)
                if not nb.first:
                    pool.wait_ge(gate_ready, nb.quarters)
                    pool.wait_ge(exp_bias_ready, nb.index)
                pool.wait_ge(lift_raw_ready, nb.index + 1)
                pool.nop(nofuse=True)
                nc.gpsimd.tensor_scalar(lift[:, :], lift_raw[:, :], 1.0, None, ALU.max).then_inc(lift_ready, 1)
                pool.wait_ge(dot_ready, 2 * nb.tiles + 2 * T)
                pool.nop(nofuse=True)
                nc.gpsimd.tensor_scalar(s_steep[:, :], dots[:, T:2 * T], STEEP, bias_steep[:, 0:1],
                                        ALU.mult, ALU.add).then_inc(s_steep_ready, 1)

            def fix_adj(nb, q, k):
                t = WIDE * q + k
                pool.wait_ge(adj_loaded[k % 2], 8 * nb.tiles + 16 * (t // 2 + 1))
                nc.gpsimd.tensor_tensor(adj_int[:, k % 2, t * P:(t + 1) * P], adj_int[:, k % 2, t * P:(t + 1) * P],
                                        ident_i[:, :], ALU.add).then_inc(adj_fixed, 1)

            def gates(nb, q):
                g = nb.quarters + q
                pool.wait_ge(d_top_ready, g + 1)
                pool.nop(nofuse=True)
                nc.gpsimd.tensor_scalar(d_max[:, :], d_top[:, :], TINY, 1.0 / ROW_SCALE,
                                        ALU.add, ALU.mult).then_inc(d_max_ready, 1)
                pool.wait_ge(d_max_ready, g + 1)
                pool.wait_ge(s_steep_ready, nb.index + 1)
                pool.nop(nofuse=True)
                nc.gpsimd.tensor_scalar(w_low[:, :], d_max[:, :], SLOPE, None, ALU.mult).then_inc(w_parts_ready, 1)
                nc.gpsimd.tensor_scalar(w_high[:, :], d_max[:, :], STEEP, None, ALU.mult).then_inc(w_parts_ready, 1)
                pool.wait_ge(w_parts_ready, 2 * (g + 1))
                nc.gpsimd.tensor_tensor(w_sum[:, :], w_high[:, :], s_steep[:, WIDE * q:WIDE * (q + 1)],
                                        ALU.add).then_inc(w_sum_ready, 1)
                pool.wait_ge(w_sum_ready, g + 1)
                pool.nop(nofuse=True)
                nc.gpsimd.tensor_scalar(w_pos[:, :], w_sum[:, :], 0.0, None, ALU.max).then_inc(w_pos_ready, 1)
                pool.wait_ge(w_pos_ready, g + 1)
                nc.gpsimd.tensor_tensor(w_max[:, :], w_low[:, :], w_pos[:, :], ALU.add).then_inc(w_max_ready, 1)
                pool.wait_ge(w_max_ready, g + 1)
                pool.wait_ge(lift_ready, nb.index + 1)
                if not known_below(g, 1):
                    pool.wait_ge(gate_diag_ready, g)
                pool.nop(nofuse=True)
                nc.gpsimd.tensor_scalar(gate[:, :], w_max[:, :], lift[:, 0:1], -1.0 / TINY,
                                        ALU.add, ALU.mult).then_inc(gate_ready, 1)

            def add_x(b, q, w):
                g = b.quarters + q
                pool.wait_ge(acc_read[w], g + 2)
                pool.wait_ge(x_res_loaded[w], 16 * g + 16)
                nc.gpsimd.tensor_tensor(out_sb[:, w, 0:MAIN], out_sb[:, w, 0:MAIN], x_res[:, w, 0:MAIN],
                                        ALU.add).then_inc(x_added[w], 1)

            for t in range(T + 1):
                if t < T:
                    norm_scalars(first, t)
                if t > 0:
                    norm_low(first, t - 1)
                for k in range(WIDE):
                    if t == FIRST_MASK[k] - 2:
                        fix_adj(first, 0, k)
            d_low_diagonal(first)
            batch_scalars(first)
            gates(first, 0)

            def steps(b, after):
                for s in range(STEPS):
                    q = s // T
                    for p in range(Q):
                        nq, nb = (p + 1, b) if p < Q - 1 else (0, after)
                        if nb:
                            for k in range(WIDE):
                                if s == max(MASK_STEP[p][k] - 2, 0):
                                    fix_adj(nb, nq, k)
                            if s == GATE_STEP[p]:
                                gates(nb, nq)
                    if s % T == 0 and q > 0:
                        add_x(b, q - 1, 1)
                        add_x(b, q - 1, 3)
                    if after:
                        done = NORM_STEP.index(s - 2) if s - 2 in NORM_STEP else None
                        if done is not None:
                            norm_products(after, done)
                        if s in NORM_STEP:
                            norm_scalars(after, NORM_STEP.index(s))
                        if done is not None:
                            norm_low(after, done)
                        if s == ROWS_STEP:
                            d_low_diagonal(after)
                        if s == D_MIN_STEP:
                            batch_scalars(after)
                add_x(b, Q - 1, 1)
                add_x(b, Q - 1, 3)

            over_batches(pool, steps)

        @block.scalar
        def _(act):
            def normalise(nb, t):
                n = nb.tiles + t
                act.wait_ge(x_norm_loaded[t % 4], 4 * nb.tiles + 16 * (t // 4 + 1))
                act.wait_ge(shift_ready, n + 1)
                if not known_below(n, 2):
                    act.wait_ge(h_lo_ready, n - 1)
                    if nb.first:
                        act.wait_ge(dot_ready, 2 * (n - 1))
                nc.scalar.activation(h_full[:, t % 2, :], x_norm[:, t % 4, :], ACT.Relu,
                                     bias=shift[:, t % 2:t % 2 + 1],
                                     scale=rstd[:, t % 2:t % 2 + 1]).then_inc(h_full_ready, 1)
                act.wait_ge(h_full_ready, n + 1)
                if not nb.first:
                    act.wait_ge(unit_done, nb.units - STEPS + 1)
                nc.scalar.activation(h_hi[:, nb.slot, t, 0:H], h_full[:, t % 2, :],
                                     ACT.Copy).then_inc(h_hi_ready, 1)

            def sum_products(nb, t):
                n = nb.tiles + t
                for v in range(2):
                    act.wait_ge(prod_ready, 2 * (n - T) + v + 1)
                    if t == 0 and v == 0 and not nb.first:
                        act.wait_ge(rows_turned, nb.index)
                        act.wait_ge(s_steep_ready, nb.index)
                        act.wait_ge(d_steep_ready, nb.index)
                        act.wait_ge(exp_bias_ready, nb.index)
                    nc.scalar.activation(prod_junk[:, v, :], prod[:, v, :], ACT.Copy, scale=1.0 / H_SCALE,
                                         accum_out=dots[:, v * T + t:v * T + t + 1]).then_inc(dot_ready, 1)

            def set_exp_bias(nb):
                if not nb.first:
                    act.wait_ge(prob_ready, nb.units)
                act.wait_ge(lift_ready, nb.index + 1)
                act.wait_ge(dot_ready, 2 * nb.tiles + 2 * T)
                nc.scalar.activation(exp_bias[:, :], dots[:, 0:T], ACT.Identity,
                                     bias=lift[:, 0:1]).then_inc(exp_bias_ready, 1)

            def probabilities(b, s):
                u = b.units + s
                j = s % T
                act.wait_ge(score_ready, u + 1)
                if s == 0:
                    act.wait_ge(exp_bias_ready, b.index + 1)
                nc.scalar.activation(prob[:, s % 2, :], score[:, s % 2, :], ACT.Exp,
                                     bias=exp_bias[:, j:j + 1]).then_inc(prob_ready, 1)
                act.wait_ge(prob_ready, u + 1)
                nc.scalar.activation(prob_hi[:, s % 4, :], prob[:, s % 2, :], ACT.Copy,
                                     scale=P_SCALE).then_inc(prob_hi_ready, 1)

            def scale_result(b, q, w):
                g = b.quarters + q
                act.wait_ge(inv_ready, g + 1)
                act.wait_ge(stored[w], 16 * g + 16)
                if w < WIDE - 1:
                    act.wait_ge(acc_ready, (WIDE - 1) * g + w + 1)
                else:
                    act.wait_ge(unit_done, b.units + T * (q + 1))
                nc.scalar.activation(out_sb[:, w, 0:MAIN], acc[:, w, 0:MAIN], ACT.Copy,
                                     scale=inv_sum[:, w:w + 1]).then_inc(acc_read[w], 1)

            def spread_diagonal(t):
                act.wait_ge(dot_ready, 2 * t + 1)
                if t > 1:
                    act.wait_ge(d_spread, t - 1)
                nc.scalar.activation(d_diag[:, t % 2, :], ident_f[:, :], ACT.Copy,
                                     scale=dots[:, t:t + 1]).then_inc(d_diag_ready, 1)

            def take_d_row(w):
                act.wait_ge(d_spread, WIDE * (w + 1))
                nc.scalar.activation(d_row[:, I * w:I * (w + 1)], acc[:, w, 0:I], ACT.Copy,
                                     scale=ROW_SCALE).then_inc(d_row_ready, 16 // WIDE)

            act.wait_ge(weights_loaded, 48)
            nc.scalar.activation(bias_steep[:, :], bias_b[:, :], ACT.Copy, scale=STEEP).then_inc(bias_scaled, 1)
            act.wait_ge(consts_ready, 7)
            for t in range(T + 3):
                if t < T:
                    normalise(first, t)
                if t > 2:
                    spread_diagonal(t - 3)
                    if (t - 3) % WIDE == WIDE - 1:
                        take_d_row((t - 3) // WIDE)
            set_exp_bias(first)
            for s in range(AHEAD):
                probabilities(first, s)

            def steps(b, after):
                for s in range(STEPS):
                    a = s + AHEAD
                    if a == STEPS and after:
                        set_exp_bias(after)
                    if s % T == T - 1:
                        scale_result(b, s // T, 1)
                    if a < STEPS or after:
                        probabilities(b if a < STEPS else after, a % STEPS)
                    if after:
                        for t in range(T):
                            if s == NORM_STEP[t] + 2:
                                normalise(after, t)
                            if s == SUM_STEP[t]:
                                sum_products(after, t)
                    if s % T == T - 1:
                        scale_result(b, s // T, 3)

            over_batches(act, steps)

        @block.vector
        def _(dve):
            def norm_stats(nb, t):
                n = nb.tiles + t
                dve.wait_ge(x_norm_loaded[t % 4], 4 * nb.tiles + 16 * (t // 4 + 1))
                nc.vector.bn_stats(stats[:, t % 2, :], x_norm[:, t % 4, :]).then_inc(stats_raw, 1)

            def norm_mean_var(nb, t):
                n = nb.tiles + t
                dve.wait_ge(stats_raw, n + 1)
                if not known_below(n, 2):
                    dve.wait_ge(shift_ready, n - 1)
                dve.nop(nofuse=True)
                nc.vector.bn_aggr(mean_var[:, t % 2, :], stats[:, t % 2, :]).then_inc(stats_ready, 1)

            def first_dots(t):
                dve.wait_ge(h_full_ready, t + 1)
                for v, w in enumerate((w_dst_b, w_src_b)):
                    if t > 0:
                        dve.wait_ge(dot_ready, 2 * t - 1 + v)
                    dve.nop(nofuse=True)
                    nc.vector.tensor_tensor_reduce(max_junk[:, v * H:(v + 1) * H], h_full[:, t % 2, :], w[:, :],
                                                   1.0 / H_SCALE, 0.0, ALU.mult, ALU.add,
                                                   dots[:, v * T + t:v * T + t + 1]).then_inc(dot_ready, 1)

            def take_rows(nb):
                dve.wait_ge(consts_ready, 7)
                dve.wait_ge(rows_turned, nb.index + 1)
                if not nb.first:
                    dve.wait_ge(rows_written, 16 * nb.index)
                nc.vector.tensor_scalar(rows_sb[:, :], rows_ps[0:2 * T, 0:P], row_mul[:, 0:1], row_add[:, 0:1],
                                        ALU.mult, ALU.add).then_inc(rows_ready, 1)

            def take_d_low(nb):
                dve.wait_ge(dot_ready, 2 * nb.tiles + 2 * T)
                if not nb.first:
                    dve.wait_ge(d_low_diag_ready, nb.index)
                nc.vector.tensor_reduce(d_low[:, :], dots[:, 0:T], AX.X, ALU.min).then_inc(d_low_ready, 1)

            def take_d_min(nb):
                dve.wait_ge(d_low_spread, nb.index + 1)
                if not nb.first:
                    dve.wait_ge(lift_raw_ready, nb.index)
                nc.vector.tensor_reduce(d_min[:, :], rows_ps[:, P:2 * P], AX.X, ALU.min).then_inc(d_min_ready, 1)

            def make_mask(nb, q, k):
                g = nb.quarters + q
                dve.wait_ge(adj_fixed, nb.tiles + WIDE * q + k + 1)
                if not known_below(g, 2):
                    dve.wait_ge(mask_turned, T * (g - 1) + 1)
                nc.vector.tensor_scalar(mask[:, q % 2, k, :], adj_int[:, k % 2, :], 0.0, TINY,
                                        ALU.is_equal, ALU.max).then_inc(mask_ready, 1)

            def search_mask(nb, q, k, h):
                n = nb.tiles + WIDE * q + k
                g = nb.quarters + q
                cols = slice(h * N // HALVES, (h + 1) * N // HALVES)
                if h == 0:
                    dve.wait_ge(mask_ready, n + 1)
                junk = h
                if known_below(n, WIDE):
                    junk = k % HALVES
                    dve.wait_ge(d_row_ready, 16 * (h + 1) // HALVES)
                    dve.wait_ge(dot_ready, 2 * T)
                    if k > 1 or h:
                        dve.wait_ge(part_ready, WIDE * h + k - 1)
                else:
                    if h == 0:
                        dve.wait_ge(d_row_ready, 16 * (nb.index + 1))
                    dve.wait_ge(part_ready, HALVES * n + h - 1)
                    if k == 0:
                        dve.wait_ge(d_top_ready, g)
                dve.nop(nofuse=True)
                nc.vector.tensor_tensor_reduce(max_junk[:, junk * N // HALVES:(junk + 1) * N // HALVES],
                                               d_row[:, cols], mask[:, q % 2, k, cols], 1.0,
                                               LOWEST, ALU.subtract, ALU.max,
                                               d_part[:, h, k:k + 1]).then_inc(part_ready, 1)

            def join_parts(nb, q):
                g = nb.quarters + q
                dve.wait_ge(part_ready, HALVES * WIDE * (g + 1))
                if not known_below(g, 1):
                    dve.wait_ge(d_max_ready, g)
                nc.vector.tensor_tensor(d_top[:, :], d_part[:, 0, :], d_part[:, 1, :],
                                        ALU.max).then_inc(d_top_ready, 1)

            def set_d_steep(nb):
                if not nb.first:
                    dve.wait_ge(score_ready, nb.units)
                dve.wait_ge(dot_ready, 2 * nb.tiles + 2 * T)
                nc.vector.tensor_scalar(d_steep[:, :], dots[:, 0:T], -STEEP, None,
                                        ALU.mult).then_inc(d_steep_ready, 1)

            def scores(b, s):
                u = b.units + s
                q, j = s // T, s % T
                if s == 0:
                    dve.wait_ge(d_steep_ready, b.index + 1)
                if j == 0:
                    dve.wait_ge(s_row_loaded[q % 2], 8 * b.quarters + 16 * (q // 2 + 1))
                dve.wait_ge(mask_turned, u + 1)
                nc.vector.scalar_tensor_tensor(score[:, s % 2, :], s_row[:, q % 2, :], d_steep[:, j:j + 1],
                                               gate_ps[s % 2][:, 0:I], ALU.max, ALU.add).then_inc(score_ready, 1)

            def low_halves(b, s):
                u = b.units + s
                dve.wait_ge(prob_hi_ready, u + 1)
                nc.vector.scalar_tensor_tensor(prob_lo[:, s % 4, :], prob[:, s % 2, :], P_SCALE,
                                               prob_hi[:, s % 4, :], ALU.mult,
                                               ALU.subtract).then_inc(prob_lo_ready, 1)

            def take_rest(b, q):
                g = b.quarters + q
                dve.wait_ge(rest_ready, g + 1)
                dve.wait_ge(rest_added, g + 1)
                for w in range(1, WIDE, 2):
                    dve.wait_ge(acc_read[w], g + 1)
                columns = acc_rest[:, 0:WIDE * (REST + 1)].rearrange("p (w c) -> p w c", w=WIDE)
                nc.vector.reciprocal(inv_sum[:, :], columns[:, :, REST]).then_inc(inv_ready, 1)
                nc.vector.tensor_copy(rest_sb[:, :, :], columns[:, :, 0:REST]).then_inc(rest_read, 1)

            def finish(b, q, w):
                g = b.quarters + q
                dve.wait_ge(acc_ready, (WIDE - 1) * g + w + 1)
                dve.wait_ge(inv_ready, g + 1)
                dve.wait_ge(x_res_loaded[w], 16 * g + 16)
                dve.wait_ge(stored[w], 16 * g + 16)
                nc.vector.scalar_tensor_tensor(out_sb[:, w, 0:MAIN], acc[:, w, 0:MAIN], inv_sum[:, w:w + 1],
                                               x_res[:, w, 0:MAIN], ALU.mult, ALU.add).then_inc(acc_read[w], 1)

            def finish_rest(b, q):
                g = b.quarters + q
                dve.wait_ge(rest_read, g + 2)
                for w in range(WIDE):
                    if w % 2:
                        dve.wait_ge(x_res_loaded[w], 16 * g + 16)
                        dve.wait_ge(stored[w], 16 * g + 16)
                    last = nc.vector.scalar_tensor_tensor(out_sb[:, w, MAIN:H], rest_sb[:, w, 0:REST],
                                                          inv_sum[:, w:w + 1], x_res[:, w, MAIN:H],
                                                          ALU.mult, ALU.add)
                last.then_inc(rest_added, 1)

            def diagonals(nb, q):
                g = nb.quarters + q
                dve.wait_ge(gate_ready, g + 1)
                if not known_below(g, 2):
                    dve.wait_ge(mask_turned, T * (g - 1) + 1)
                for k in range(WIDE):
                    last = nc.vector.tensor_scalar(gate_diag[:, q % 2, k, :], ident_b[:, :], gate[:, k:k + 1],
                                                   None, ALU.mult)
                last.then_inc(gate_diag_ready, 1)

            dve.sem_inc(rest_read, 1)
            dve.sem_inc(rest_added, 1)
            for w in range(WIDE):
                dve.sem_inc(acc_read[w], 1)
                dve.sem_inc(stored[w], 16)
            for t in range(T + 2):
                if t < T:
                    norm_stats(first, t)
                if t == 2:
                    dve.wait_ge(weights_loaded, 48)
                if t > 1:
                    first_dots(t - 2)
                if t < T:
                    norm_mean_var(first, t)
                for k in range(WIDE):
                    if t == FIRST_MASK[k]:
                        make_mask(first, 0, k)
            for k in range(WIDE):
                search_mask(first, 0, k, 0)
                if k == 0:
                    take_d_low(first)
                if k == 1:
                    take_rows(first)
                    set_d_steep(first)
            take_d_min(first)
            for k in range(WIDE):
                search_mask(first, 0, k, 1)
            join_parts(first, 0)
            diagonals(first, 0)
            scores(first, 0)
            scores(first, 1)
            low_halves(first, 0)

            def steps(b, after):
                for s in range(STEPS):
                    q = s // T
                    a = s + AHEAD
                    if a == STEPS and after:
                        set_d_steep(after)
                    if a < STEPS or after:
                        scores(b if a < STEPS else after, a % STEPS)
                    if s % T == T - 1:
                        take_rest(b, q)
                    if a - 1 < STEPS or after:
                        low_halves(b if a - 1 < STEPS else after, (a - 1) % STEPS)
                    if s % T == T - 1:
                        finish(b, q, 0)
                        finish(b, q, 2)
                    if s % T == 0 and q > 0:
                        finish_rest(b, q - 1)
                    if after:
                        for t in range(T):
                            if s == NORM_STEP[t]:
                                norm_stats(after, t)
                        if s == ROWS_STEP:
                            take_rows(after)
                            take_d_low(after)
                        if s == D_MIN_STEP:
                            take_d_min(after)
                    for p in range(Q):
                        nq, nb = (p + 1, b) if p < Q - 1 else (0, after)
                        if nb:
                            for k in range(WIDE):
                                if s == MASK_STEP[p][k]:
                                    make_mask(nb, nq, k)
                                for h in range(HALVES):
                                    if s == TOP_STEP[p][k][h]:
                                        search_mask(nb, nq, k, h)
                            if s == GATE_STEP[p]:
                                join_parts(nb, nq)
                            if s == GATE_STEP[p] + 2:
                                diagonals(nb, nq)
                    if after:
                        for t in range(T):
                            if s == NORM_STEP[t]:
                                norm_mean_var(after, t)
                finish_rest(b, Q - 1)

            over_batches(dve, steps)

        @block.tensor
        def _(pe):
            def turn_rows(nb):
                pe.wait_ge(dot_ready, 2 * nb.tiles + 2 * T)
                if not nb.first:
                    pe.wait_ge(d_min_ready, nb.index)
                nc.tensor.transpose(rows_ps[0:2 * T, 0:P], dots[:, :], ident_f[:, :]).then_inc(rows_turned, 1)

            def spread_d_low(nb):
                pe.wait_ge(d_low_diag_ready, nb.index + 1)
                pe.wait_ge(rows_ready, nb.index + 1)
                nc.tensor.matmul(rows_ps[:, P:2 * P], ones_f[:, :], d_low_diag[:, :],
                                 start=True, stop=True).then_inc(d_low_spread, 1)

            def turn_masks(b, s):
                u = b.units + s
                q, j = s // T, s % T
                if j == 0:
                    pe.wait_ge(gate_diag_ready, b.quarters + q + 1)
                    pe.wait_ge(mask_ready, b.tiles + WIDE * (q + 1))
                for k in range(WIDE):
                    last = nc.tensor.matmul(gate_ps[s % 2][:, k * P:(k + 1) * P],
                                            mask[:, q % 2, k, j * P:(j + 1) * P], gate_diag[:, q % 2, k, :],
                                            start=True, stop=True)
                last.then_inc(mask_turned, 1)

            def multiply(b, s):
                u = b.units + s
                q, j = s // T, s % T
                if s == 0:
                    pe.wait_ge(h_lo_ready, b.tiles + T)
                hi = h_hi[:, b.slot, j, :]
                lo = h_lo[:, b.slot, j, :]
                start, stop = j == 0, j == T - 1
                if start:
                    pe.wait_ge(rest_read, b.quarters + q + 1)
                for w in range(WIDE):
                    p_hi = prob_hi[:, s % 4, w * P:(w + 1) * P]
                    p_lo = prob_lo[:, s % 4, w * P:(w + 1) * P]
                    c = w * (REST + 1)
                    rest = acc_rest[:, c:c + REST + 1]
                    nc.tensor.matmul(rest, p_hi, hi[:, MAIN:H + 1], start=start and w == 0, stop=False,
                                     skip_group_check=True)
                    nc.tensor.matmul(acc_rest[:, c:c + REST], p_hi, lo[:, MAIN:H], start=False, stop=False,
                                     skip_group_check=True)
                    last = nc.tensor.matmul(rest, p_lo, hi[:, MAIN:H + 1], start=False, stop=stop,
                                            skip_group_check=True)
                if stop:
                    last.then_inc(rest_ready, 1)
                for w in range(WIDE):
                    if start:
                        pe.wait_ge(acc_read[w], b.quarters + q + 1)
                    p_hi = prob_hi[:, s % 4, w * P:(w + 1) * P]
                    p_lo = prob_lo[:, s % 4, w * P:(w + 1) * P]
                    main = acc[:, w, 0:MAIN]
                    nc.tensor.matmul(main, p_hi, hi[:, 0:MAIN], start=start, stop=False)
                    nc.tensor.matmul(main, p_hi, lo[:, 0:MAIN], start=False, stop=False)
                    last = nc.tensor.matmul(main, p_lo, hi[:, 0:MAIN], start=False, stop=stop)
                    if stop and w < WIDE - 1:
                        last.then_inc(acc_ready, 1)
                last.then_inc(unit_done, 1)

            pe.wait_ge(consts_ready, 7)
            for t in range(T):
                pe.wait_ge(d_diag_ready, t + 1)
                nc.tensor.matmul(acc[:, t // WIDE, P * (t % WIDE):P * (t % WIDE + 1)], ones_f[:, :],
                                 d_diag[:, t % 2, :], start=True, stop=True).then_inc(d_spread, 1)
            turn_rows(first)
            spread_d_low(first)
            turn_masks(first, 0)
            turn_masks(first, 1)

            def steps(b, after):
                for s in range(STEPS):
                    a = s + AHEAD
                    if s == ROWS_STEP and after:
                        turn_rows(after)
                    if s == D_MIN_STEP and after:
                        spread_d_low(after)
                    pe.wait_ge(prob_lo_ready, b.units + s + 1)
                    if a < STEPS or after:
                        turn_masks(b if a < STEPS else after, a % STEPS)
                    multiply(b, s)

            over_batches(pe, steps)


_INS = ["x", "adj", "L0_gnn_attn_w_src", "L0_gnn_attn_w_dst", "L0_gnn_attn_b"]


def kernel(**inputs):
    import numpy as _np
    import concourse.bacc as _bacc
    from concourse import mybir as _mybir
    from concourse.bass_utils import run_bass_kernel_spmd as _run

    nc = _bacc.Bacc("TRN2", target_bir_lowering=False, num_devices=1)
    arrays, args = {}, []
    for name in _INS:
        a = _np.ascontiguousarray(inputs[name])
        arrays[f"in_{name}_dram"] = a
        args.append(nc.dram_tensor(f"in_{name}_dram", a.shape, _mybir.dt.from_np(a.dtype), kind="ExternalInput").ap())
    x = arrays["in_x_dram"]
    args.append(nc.dram_tensor("out_0_dram", x.shape, _mybir.dt.from_np(x.dtype), kind="ExternalOutput").ap())
    gnn_layer(nc, *args)
    r = _run(nc, [arrays], core_ids=[0])
    return r.results[0]["out_0_dram"]
```
